# Optimizing a Trainium2 kernel written in Bass

```python
import numpy as np
import jax
import jax.numpy as jnp

def _softmax(x, axis=-1):
    return jax.nn.softmax(x, axis=axis)

def _gelu(x):
    return jax.nn.gelu(x, approximate=True)

def _silu(x):
    return jax.nn.silu(x)

def _sigmoid(x):
    return jax.nn.sigmoid(x)

def _layernorm(x, axis=-1, eps=1e-05):
    m = jnp.mean(x, axis=axis, keepdims=True)
    v = jnp.var(x, axis=axis, keepdims=True)
    return (x - m) / jnp.sqrt(v + eps)

def _scatter_add(tgt, idx, src, axis=0):
    return tgt.at[idx].add(src)

def _segment_sum(src, seg, n):
    return jax.ops.segment_sum(src, seg, n)
kernel_name = 'mk_dlrm_tower_d1_rec_r8_ab8b57'

def setup_inputs(seed: int=0):
    np.random.seed(seed)
    _w = jnp.asarray

    def _rec_inputs():
        import jax
        import jax.numpy as jnp
        _tk = jax.random.key(seed)
        dense_ctx = jax.random.normal(jax.random.fold_in(_tk, 190), (1024, 16), jnp.float32)
        ids = jnp.stack([jax.random.randint(jax.random.fold_in(_tk, 200 + f), (1024,), 0, v, jnp.int32) for f, v in enumerate([1000, 12500, 1250, 1000, 125000, 12500, 12500, 1000, 1000, 1250, 12500, 1000, 1000, 1250, 125000, 12500, 1250, 1000, 1250, 12500, 1250, 125000, 12500, 1000, 1250, 125000])], axis=1)
        tbl_0 = 0.05 * jax.random.normal(jax.random.fold_in(_tk, 500 + 0), (1000, 32), jnp.float32)
        tbl_1 = 0.05 * jax.random.normal(jax.random.fold_in(_tk, 500 + 1), (12500, 32), jnp.float32)
        tbl_2 = 0.05 * jax.random.normal(jax.random.fold_in(_tk, 500 + 2), (1250, 32), jnp.float32)
        tbl_3 = 0.05 * jax.random.normal(jax.random.fold_in(_tk, 500 + 3), (1000, 32), jnp.float32)
        tbl_4 = 0.05 * jax.random.normal(jax.random.fold_in(_tk, 500 + 4), (125000, 32), jnp.float32)
        tbl_5 = 0.05 * jax.random.normal(jax.random.fold_in(_tk, 500 + 5), (12500, 32), jnp.float32)
        tbl_6 = 0.05 * jax.random.normal(jax.random.fold_in(_tk, 500 + 6), (12500, 32), jnp.float32)
        tbl_7 = 0.05 * jax.random.normal(jax.random.fold_in(_tk, 500 + 7), (1000, 32), jnp.float32)
        tbl_8 = 0.05 * jax.random.normal(jax.random.fold_in(_tk, 500 + 8), (1000, 32), jnp.float32)
        tbl_9 = 0.05 * jax.random.normal(jax.random.fold_in(_tk, 500 + 9), (1250, 32), jnp.float32)
        tbl_10 = 0.05 * jax.random.normal(jax.random.fold_in(_tk, 500 + 10), (12500, 32), jnp.float32)
        tbl_11 = 0.05 * jax.random.normal(jax.random.fold_in(_tk, 500 + 11), (1000, 32), jnp.float32)
        tbl_12 = 0.05 * jax.random.normal(jax.random.fold_in(_tk, 500 + 12), (1000, 32), jnp.float32)
        tbl_13 = 0.05 * jax.random.normal(jax.random.fold_in(_tk, 500 + 13), (1250, 32), jnp.float32)
        tbl_14 = 0.05 * jax.random.normal(jax.random.fold_in(_tk, 500 + 14), (125000, 32), jnp.float32)
        tbl_15 = 0.05 * jax.random.normal(jax.random.fold_in(_tk, 500 + 15), (12500, 32), jnp.float32)
        tbl_16 = 0.05 * jax.random.normal(jax.random.fold_in(_tk, 500 + 16), (1250, 32), jnp.float32)
        tbl_17 = 0.05 * jax.random.normal(jax.random.fold_in(_tk, 500 + 17), (1000, 32), jnp.float32)
        tbl_18 = 0.05 * jax.random.normal(jax.random.fold_in(_tk, 500 + 18), (1250, 32), jnp.float32)
        tbl_19 = 0.05 * jax.random.normal(jax.random.fold_in(_tk, 500 + 19), (12500, 32), jnp.float32)
        tbl_20 = 0.05 * jax.random.normal(jax.random.fold_in(_tk, 500 + 20), (1250, 32), jnp.float32)
        tbl_21 = 0.05 * jax.random.normal(jax.random.fold_in(_tk, 500 + 21), (125000, 32), jnp.float32)
        tbl_22 = 0.05 * jax.random.normal(jax.random.fold_in(_tk, 500 + 22), (12500, 32), jnp.float32)
        tbl_23 = 0.05 * jax.random.normal(jax.random.fold_in(_tk, 500 + 23), (1000, 32), jnp.float32)
        tbl_24 = 0.05 * jax.random.normal(jax.random.fold_in(_tk, 500 + 24), (1250, 32), jnp.float32)
        tbl_25 = 0.05 * jax.random.normal(jax.random.fold_in(_tk, 500 + 25), (125000, 32), jnp.float32)
        _rk = jax.random.fold_in(_tk, 7)
        W_top1 = 0.0606339 * jax.random.normal(jax.random.fold_in(_tk, 801), (272, 512), jnp.float32)
        W_top2 = 0.0441942 * jax.random.normal(jax.random.fold_in(_tk, 802), (512, 256), jnp.float32)
        W_top3 = 0.0625 * jax.random.normal(jax.random.fold_in(_tk, 803), (256, 1), jnp.float32)
        b_top1 = jnp.zeros((512,), jnp.float32)
        b_top2 = jnp.zeros((256,), jnp.float32)
        return (dense_ctx, ids, tbl_0, tbl_1, tbl_2, tbl_3, tbl_4, tbl_5, tbl_6, tbl_7, tbl_8, tbl_9, tbl_10, tbl_11, tbl_12, tbl_13, tbl_14, tbl_15, tbl_16, tbl_17, tbl_18, tbl_19, tbl_20, tbl_21, tbl_22, tbl_23, tbl_24, tbl_25, W_top1, b_top1, W_top2, b_top2, W_top3)
    dense_ctx, ids, tbl_0, tbl_1, tbl_2, tbl_3, tbl_4, tbl_5, tbl_6, tbl_7, tbl_8, tbl_9, tbl_10, tbl_11, tbl_12, tbl_13, tbl_14, tbl_15, tbl_16, tbl_17, tbl_18, tbl_19, tbl_20, tbl_21, tbl_22, tbl_23, tbl_24, tbl_25, W_top1, b_top1, W_top2, b_top2, W_top3 = _rec_inputs()

    def _L0_rec_setup():
        import jax, jax.numpy as jnp
        import numpy as np
        M_FIELDS = 26
        H1 = 128
        H2 = 128
        BATCH = 256
        EMB_K = 32

        def _cin_layer(x_prev, x0, W, b):
            return jnp.einsum('bik,bjk,hij->bhk', x_prev, x0, W) + b[None, :, None]
        key = jax.random.key(seed)
        k0, k1, k2, k3, k4 = jax.random.split(key, 5)
        inputs = jax.random.normal(k0, (BATCH, M_FIELDS, EMB_K), dtype=jnp.float32)
        W1 = jax.random.normal(k1, (H1, M_FIELDS, M_FIELDS), dtype=jnp.float32) * 0.05
        b1 = jax.random.normal(k2, (H1,), dtype=jnp.float32) * 0.05
        W2 = jax.random.normal(k3, (H2, H1, M_FIELDS), dtype=jnp.float32) * 0.05
        b2 = jax.random.normal(k4, (H2,), dtype=jnp.float32) * 0.05
        return {'inputs': inputs, 'W1': W1, 'b1': b1, 'W2': W2, 'b2': b2}
    _L0_rec_all = _L0_rec_setup()
    _L0_rec_in = {k: v for k, v in _L0_rec_all.items() if k in ('W1', 'b1', 'W2', 'b2')}
    del _L0_rec_all
    return {'dense_ctx': dense_ctx, 'ids': ids, 'tbl_0': tbl_0, 'tbl_1': tbl_1, 'tbl_2': tbl_2, 'tbl_3': tbl_3, 'tbl_4': tbl_4, 'tbl_5': tbl_5, 'tbl_6': tbl_6, 'tbl_7': tbl_7, 'tbl_8': tbl_8, 'tbl_9': tbl_9, 'tbl_10': tbl_10, 'tbl_11': tbl_11, 'tbl_12': tbl_12, 'tbl_13': tbl_13, 'tbl_14': tbl_14, 'tbl_15': tbl_15, 'tbl_16': tbl_16, 'tbl_17': tbl_17, 'tbl_18': tbl_18, 'tbl_19': tbl_19, 'tbl_20': tbl_20, 'tbl_21': tbl_21, 'tbl_22': tbl_22, 'tbl_23': tbl_23, 'tbl_24': tbl_24, 'tbl_25': tbl_25, 'W_top1': W_top1, 'b_top1': b_top1, 'W_top2': W_top2, 'b_top2': b_top2, 'W_top3': W_top3, 'L0_rec_W1': _L0_rec_in['W1'], 'L0_rec_b1': _L0_rec_in['b1'], 'L0_rec_W2': _L0_rec_in['W2'], 'L0_rec_b2': _L0_rec_in['b2']}

def reference(dense_ctx, ids, tbl_0, tbl_1, tbl_2, tbl_3, tbl_4, tbl_5, tbl_6, tbl_7, tbl_8, tbl_9, tbl_10, tbl_11, tbl_12, tbl_13, tbl_14, tbl_15, tbl_16, tbl_17, tbl_18, tbl_19, tbl_20, tbl_21, tbl_22, tbl_23, tbl_24, tbl_25, W_top1, b_top1, W_top2, b_top2, W_top3, L0_rec_W1, L0_rec_b1, L0_rec_W2, L0_rec_b2):
    import jax
    import jax.numpy as jnp

    def _L0_rec_ref(inputs, W1, b1, W2, b2):
        import jax, jax.numpy as jnp
        import numpy as np
        M_FIELDS = 26
        H1 = 128
        H2 = 128
        BATCH = 256
        EMB_K = 32

        def _cin_layer(x_prev, x0, W, b):
            return jnp.einsum('bik,bjk,hij->bhk', x_prev, x0, W) + b[None, :, None]
        x1 = _cin_layer(inputs, inputs, W1, b1)
        x2 = _cin_layer(x1, inputs, W2, b2)
        res = jnp.concatenate([x1, x2], axis=1)
        return jnp.sum(res, axis=-1)
    e = jnp.stack([tbl_0[ids[:, 0]], tbl_1[ids[:, 1]], tbl_2[ids[:, 2]], tbl_3[ids[:, 3]], tbl_4[ids[:, 4]], tbl_5[ids[:, 5]], tbl_6[ids[:, 6]], tbl_7[ids[:, 7]], tbl_8[ids[:, 8]], tbl_9[ids[:, 9]], tbl_10[ids[:, 10]], tbl_11[ids[:, 11]], tbl_12[ids[:, 12]], tbl_13[ids[:, 13]], tbl_14[ids[:, 14]], tbl_15[ids[:, 15]], tbl_16[ids[:, 16]], tbl_17[ids[:, 17]], tbl_18[ids[:, 18]], tbl_19[ids[:, 19]], tbl_20[ids[:, 20]], tbl_21[ids[:, 21]], tbl_22[ids[:, 22]], tbl_23[ids[:, 23]], tbl_24[ids[:, 24]], tbl_25[ids[:, 25]]], axis=1)
    z = _L0_rec_ref(e, L0_rec_W1, L0_rec_b1, L0_rec_W2, L0_rec_b2)
    z = z.reshape(z.shape[0], -1)
    h = jnp.concatenate([z, dense_ctx], axis=1)
    h = jnp.maximum(h @ W_top1 + b_top1, 0.0)
    h = jnp.maximum(h @ W_top2 + b_top2, 0.0)
    y = h @ W_top3
    return y

_drawn_inputs = setup_inputs


def setup_inputs(seed=0):
    import zlib

    import numpy as np

    out = dict(_drawn_inputs(seed))
    spreads = {'b_top1': (0.0, 2.0), 'b_top2': (0.0, 0.8)}
    factors = {'tbl_0': 8.0,
     'tbl_1': 8.0,
     'tbl_2': 8.0,
     'tbl_3': 8.0,
     'tbl_4': 8.0,
     'tbl_5': 8.0,
     'tbl_6': 8.0,
     'tbl_7': 8.0,
     'tbl_8': 8.0,
     'tbl_9': 8.0,
     'tbl_10': 8.0,
     'tbl_11': 8.0,
     'tbl_12': 8.0,
     'tbl_13': 8.0,
     'tbl_14': 8.0,
     'tbl_15': 8.0,
     'tbl_16': 8.0,
     'tbl_17': 8.0,
     'tbl_18': 8.0,
     'tbl_19': 8.0,
     'tbl_20': 8.0,
     'tbl_21': 7.646,
     'tbl_22': 8.0,
     'tbl_23': 8.0,
     'tbl_24': 8.0,
     'tbl_25': 8.0,
     'L0_rec_W1': 7.769,
     'L0_rec_W2': 4.122,
     'dense_ctx': 5.622}
    for name, (base, spread) in spreads.items():
        noise = np.random.default_rng([zlib.crc32(name.encode()), seed]).standard_normal(out[name].shape)
        drawn = base * np.exp(spread * noise) if base else spread * noise
        out[name] = jnp.asarray(drawn.astype(out[name].dtype))
    for name, factor in factors.items():
        out[name] = (out[name] * factor).astype(out[name].dtype)
    return out
```

```python
import concourse.bass as bass
from concourse import mybir
from contextlib import ExitStack

F32 = mybir.dt.float32
I32 = mybir.dt.int32
ALU = mybir.AluOpType
ACT = mybir.ActivationFunctionType

BATCH, FIELDS, K, H = 1024, 26, 32, 128
DENSE, TOP1, TOP2 = 16, 512, 256
P = 128
TILES = BATCH // P
Q = P // K
R = P // Q
HALVES, RH = 2, R // 2

SMALL = 5
SPLIT = 12
ONE_ROWS = 1 + SMALL


def small_row(a):
    return ONE_ROWS + sum(SMALL - x for x in range(a))


def large_row(p):
    lo, base = (SPLIT, small_row(SMALL)) if p >= SPLIT else (SMALL, 0)
    return base + sum(FIELDS - x for x in range(lo, p))


ROWS = large_row(FIELDS - 1) + 1
assert ROWS == large_row(SPLIT - 1) + FIELDS - SPLIT + 1 == 126
COLS = (1 + FIELDS, 1 + SPLIT)
UNIT0 = (0, COLS[0])
CROSS = COLS[0] + COLS[1]
UNITS = CROSS + 1
LARGE = FIELDS - SMALL
CROSS_ROWS = SMALL * LARGE
Z2_UNITS = [u for u in range(CROSS) if u not in UNIT0]
Z1_UNITS = [*UNIT0, CROSS]

PAIRS = FIELDS * FIELDS
US = PAIRS + 2
BANK = 512
RPB = (4, 8)
PER_UNROLL = 2
LOOPS = TILES // PER_UNROLL
DRAINS = 12
TURNS = -(-UNITS // 4)


def dlrm_tower(nc, ids, tables, dense_t, w1, w2_t, b1, b2, wt1, bt1, wt2, bt2, wt3, out):
    with ExitStack() as ctx:
        def sb(name, shape, dt=F32):
            return ctx.enter_context(nc.sbuf_tensor(name, shape, dt))

        def sem(name):
            return ctx.enter_context(nc.semaphore(name))

        idx = [sb(f"idx{t}", [P, FIELDS], I32) for t in range(2)]
        rows = [sb(f"rows{t}", [P, FIELDS * K]) for t in range(2)]
        feats = sb("feats", [P, FIELDS, R])
        pair_mem = sb("pair_mem", [P, HALVES * RH * 2 * ROWS])
        pairs = [pair_mem[:, h * RH * 2 * ROWS:(h + 1) * RH * 2 * ROWS].rearrange(
            "p (r w) -> p r w", r=RH) for h in range(HALVES)]
        w2_sb = pair_mem[:, 0:FIELDS * H].rearrange("i (j h) -> i j h", j=FIELDS)
        w1_sb = pair_mem[:, FIELDS * H:FIELDS * H + PAIRS].rearrange("i (a b) -> i a b", a=FIELDS)
        blocks = [sb(f"blocks{t}", [P, R, COLS[0], Q]) for t in range(2)]
        u_mem = sb("u_mem", [P, FIELDS * US])
        sums = u_mem[0:ROWS, 0:CROSS * P].rearrange("w (u n) -> w u n", n=P)
        s1 = sb("s1", [P, US])
        wh = sb("wh", [P, UNITS, ROWS])
        wr = sb("wr", [ROWS, UNITS, H])
        cross = sb("cross", [CROSS_ROWS, P])
        ident = sb("ident", [P, P])
        b12 = sb("b12", [P, 2])
        b12k = sb("b12k", [P, 2])
        z_sb = sb("z_sb", [H, 2, P])
        h1_sb = sb("h1_sb", [P, TOP1 // P, P])
        h2_sb = sb("h2_sb", [P, TOP2 // P, P])
        y_sb = sb("y_sb", [1, BATCH])
        dense_sb = sb("dense_sb", [DENSE, BATCH])
        wt1_z = sb("wt1_z", [H, 2, TOP1])
        wt1_d = sb("wt1_d", [DENSE, TOP1])
        wt2_sb = sb("wt2_sb", [P, TOP1 // P, TOP2])
        wt3_sb = sb("wt3_sb", [P, TOP2 // P])
        bt1_sb = sb("bt1_sb", [P, TOP1 // P])
        bt2_sb = sb("bt2_sb", [P, TOP2 // P])

        banks = ctx.enter_context(nc.psum_tensor("banks", [P, 8, BANK], F32))
        feats_ps = banks[:, 0:2, :].rearrange("p b w -> p (b w)")[:, 0:FIELDS * R].rearrange(
            "p (f r) -> p f r", r=R)
        RING = (2, 3, 4)
        z_ps = banks[:, 5, 0:2 * P].rearrange("h (l n) -> h l n", l=2)
        h1_ps = banks[:, 6, :].rearrange("h (m n) -> h m n", n=P)
        h2_ps = banks[:, 7, 0:TOP2 // P * P].rearrange("h (m n) -> h m n", n=P)
        y_ps = banks[0:1, 7, 3 * P:4 * P]

        w_loaded = sem("w_loaded")
        top_loaded = sem("top_loaded")
        ids_loaded = [sem(f"ids_loaded{t}") for t in range(2)]
        rows_gathered = [sem(f"rows_gathered{t}") for t in range(2)]
        gather_started = sem("gather_started")
        ident_zeroed = sem("ident_zeroed")
        ident_made = sem("ident_made")
        s1_steps = sem("s1_steps")
        u_made = sem("u_made")
        u_kept = sem("u_kept")
        wh_steps = sem("wh_steps")
        feats_made = sem("feats_made")
        blocks_made = sem("blocks_made")
        blocks_free = [sem(f"blocks_free{t}") for t in range(2)]
        pairs_made = sem("pairs_made")
        bank_filled = sem("bank_filled")
        bank_drained = sem("bank_drained")
        cross_moved = sem("cross_moved")
        z_made, z_kept = sem("z_made"), sem("z_kept")
        h1_made, h1_kept = sem("h1_made"), sem("h1_kept")
        h2_made, h2_kept = sem("h2_made"), sem("h2_kept")
        y_made, y_kept = sem("y_made"), sem("y_kept")
        out_stored = sem("out_stored")

        def fill(g, t, k):
            return g * (PER_UNROLL * DRAINS) + (TURNS + t * DRAINS + k)

        def ring_bank(t, k):
            return RING[(TURNS + t * DRAINS + k) % 3]

        FILLS = [(c, r) for b in range(R // 8) for c, r in ((0, 8 * b), (0, 8 * b + 4), (1, 8 * b))]

        def u_view(j, p, q, outer, inner):
            return bass.AP(u_mem, j * US + p * FIELDS + q, [[FIELDS * US, P], list(outer), list(inner)])

        def wh_view(unit, row, outer, inner):
            return bass.AP(wh, unit * ROWS + row, [[UNITS * ROWS, P], list(outer), list(inner)])

        def triples():
            for p in range(FIELDS):
                hi = SMALL if p < SMALL else FIELDS
                chunk = 1 if SMALL <= p < SPLIT else 0
                row = small_row(p) if p < SMALL else large_row(p)
                x, z = p + 1, hi - p
                yield (wh_view(UNIT0[chunk] + 1, row, (ROWS, x), (1, z)),
                       u_view(0, p, p, (US, x), (1, z)),
                       u_view(p, p, 0, (1, x), (FIELDS, z)),
                       u_view(p, 0, p, (FIELDS, x), (US, z)))
            for a in range(SMALL):
                y = SMALL - a
                yield (wh_view(1 + SMALL, small_row(a), (ROWS, LARGE), (1, y)),
                       u_view(a, a, SMALL, (1, LARGE), (FIELDS, y)),
                       u_view(a, SMALL, a, (FIELDS, LARGE), (US, y)),
                       u_view(SMALL, a, a, (US, LARGE), (1, y)))

        block = ctx.enter_context(nc.Block())

        @block.sync
        def _(sp):
            sp.dma_start(idx[0][:, :], ids[0:P, :]).then_inc(ids_loaded[0], 16)
            sp.dma_start(w1_sb.rearrange("i a b -> i (a b)"), w1).then_inc(w_loaded, 16)
            sp.dma_start(w2_sb.rearrange("i j h -> i (j h)"), w2_t).then_inc(w_loaded, 16)
            sp.dma_start(b12[:, 0:1], b1).then_inc(w_loaded, 16)
            sp.dma_start(b12[:, 1:2], b2).then_inc(w_loaded, 16)
            sp.dma_start(idx[1][:, :], ids[P:2 * P, :]).then_inc(ids_loaded[1], 16)
            sp.dma_start(dense_sb[:, :], dense_t).then_inc(top_loaded, 16)
            sp.dma_start(wt1_z[:, :, :], wt1[0:2 * H, :].rearrange("(l h) n -> h l n", l=2)).then_inc(top_loaded, 16)
            sp.dma_start(wt1_d[:, :], wt1[2 * H:2 * H + DENSE, :]).then_inc(top_loaded, 16)
            sp.dma_start(wt2_sb[:, :, :], wt2.rearrange("(m h) n -> h m n", h=P)).then_inc(top_loaded, 16)
            sp.dma_start(wt3_sb[:, :], wt3).then_inc(top_loaded, 16)
            sp.dma_start(bt1_sb[:, :], bt1).then_inc(top_loaded, 16)
            sp.dma_start(bt2_sb[:, :], bt2).then_inc(top_loaded, 16)

            def move_cross(g, t):
                sp.wait_ge(bank_drained, fill(g, t + 1, 0))
                for s in range(SMALL):
                    sp.dma_start(cross[s * LARGE:(s + 1) * LARGE, :],
                                 sums[1 + s:2 + s, 1 + SMALL:1 + FIELDS, :]).then_inc(cross_moved, 16)

            with sp.Fori(0, LOOPS - 1) as g:
                for t in range(PER_UNROLL):
                    sp.wait_ge(feats_made, g * 2 + (t + 1))
                    sp.dma_start(idx[t][:, :], ids[bass.ds((g + 1) * (2 * P) + t * P, P), :]).then_inc(ids_loaded[t], 16)
                    move_cross(g, t)
            for t in range(PER_UNROLL):
                move_cross(LOOPS - 1, t)
            sp.wait_ge(y_kept, TILES)
            sp.dma_start(out, y_sb[:, :]).then_inc(out_stored, 16)
            sp.wait_ge(out_stored, 16)

        @block.gpsimd
        def _(pool):
            pool.memset(ident[:, :], 0.0).then_inc(ident_zeroed, 1)
            pool.wait_ge(ident_zeroed, 1)
            pool.affine_select(out=ident[:, :], in_=ident[:, :], compare_op=ALU.not_equal, fill=1.0,
                               base=0, pattern=[[-1, P]], channel_multiplier=1).then_inc(ident_made, 1)
            with pool.Fori(0, LOOPS) as g:
                for t in range(PER_UNROLL):
                    pool.wait_ge(ids_loaded[t], (g + 1) * 16)
                    pool.sem_inc(gather_started, 1)
                    for f in range(FIELDS):
                        pool.indirect_dma_start(
                            rows[t][:, f * K:(f + 1) * K], None, tables[f],
                            bass.IndirectOffsetOnAxis(ap=idx[t][:, f:f + 1], axis=0),
                        ).then_inc(rows_gathered[t], 16)

        @block.vector
        def _(dve):
            dve.wait_ge(w_loaded, 64)
            s1_ab = s1[:, 0:PAIRS].rearrange("i (a b) -> i a b", a=FIELDS)
            dve.tensor_tensor(s1_ab, w1_sb, w1_sb.rearrange("i a b -> i b a"), ALU.add).then_inc(s1_steps, 1)
            dve.memset(s1[:, PAIRS + 1:US], 0.0)
            dve.tensor_copy(s1[:, PAIRS:PAIRS + 1], b12[:, 0:1])
            dve.wait_ge(s1_steps, 1)
            dve.tensor_copy(s1[:, 0:PAIRS:FIELDS + 1],
                            w1_sb.rearrange("i a b -> i (a b)")[:, 0:PAIRS:FIELDS + 1]).then_inc(s1_steps, 1)
            dve.tensor_scalar(b12k[:, :], b12[:, :], float(K), None, ALU.mult)
            dve.memset(wh[:, :, :].rearrange("h u w -> h (u w)"), 0.0).then_inc(wh_steps, 1)
            for t in range(2):
                dve.memset(blocks[t][:, :, :, :].rearrange("p r c q -> p (r c q)"), 0.0).then_inc(wh_steps, 1)
            dve.wait_ge(wh_steps, 3)
            for t in range(2):
                for q in range(Q):
                    last = dve.memset(blocks[t][q * K:(q + 1) * K, :, 0, q], 1.0)
                last.then_inc(blocks_free[t], 1)

            dve.wait_ge(s1_steps, 2)
            for p in range(FIELDS):
                hi = SMALL if p < SMALL else FIELDS
                chunk = 1 if SMALL <= p < SPLIT else 0
                row = small_row(p) if p < SMALL else large_row(p)
                dve.tensor_copy(wh[:, UNIT0[chunk], row:row + hi - p], s1_ab[:, p, p:hi])
            dve.tensor_copy(wh[:, CROSS, 0:CROSS_ROWS].rearrange("h (s q) -> h s q", s=SMALL),
                            s1_ab[:, 0:SMALL, SMALL:FIELDS]).then_inc(wh_steps, 1)

            dve.wait_ge(u_kept, FIELDS)
            dve.tensor_copy(wh_view(1, 0, (ROWS, FIELDS), (1, 1)), u_view(0, 0, PAIRS, (US, FIELDS), (1, 1)))
            for to, first, _, _ in triples():
                last = dve.tensor_copy(to, first)
            last.then_inc(wh_steps, 1)
            dve.wait_ge(wh_steps, 5)
            dve.memset(u_view(0, 0, 0, (US + 1, FIELDS), (FIELDS, FIELDS)), 0.0).then_inc(wh_steps, 1)
            dve.wait_ge(wh_steps, 6)
            for to, _, second, _ in triples():
                last = dve.tensor_tensor(to, to, second, ALU.add)
            last.then_inc(wh_steps, 1)
            dve.wait_ge(wh_steps, 7)
            for to, _, _, third in triples():
                last = dve.tensor_tensor(to, to, third, ALU.add)
            last.then_inc(wh_steps, 1)

            for h in range(HALVES):
                dve.memset(pairs[h][:, :, 0], 1.0).then_inc(pairs_made, 1)

            with dve.Fori(0, LOOPS) as g:
                for t in range(PER_UNROLL):
                    dve.wait_ge(rows_gathered[t], (g + 1) * (16 * FIELDS))
                    dve.wait_ge(pairs_made, g * 4 + (2 * t + HALVES))
                    dve.transpose(feats[:, :, :].rearrange("p f r -> p (f r)"), rows[t][:, :])
                    dve.transpose(feats_ps.rearrange("p f r -> p (f r)"), rows[t][:, :]).then_inc(feats_made, 1)
                    dve.wait_ge(feats_made, g * 2 + (t + 1))
                    dve.wait_ge(blocks_free[t], g + 1)
                    for q in range(Q):
                        part = slice(q * K, (q + 1) * K)
                        last = dve.tensor_copy(blocks[t][part, :, 1:COLS[0], q].rearrange("p r f -> p f r"),
                                               feats_ps[part])
                    last.then_inc(blocks_made, 1)
                    for h in range(HALVES):
                        dve.wait_ge(bank_filled, fill(g, t - 1, (h + 1) * DRAINS // HALVES))
                        rs = slice(h * RH, (h + 1) * RH)

                        def rows_of(row, n):
                            return pairs[h][:, :, row:row + n].rearrange("p r w -> p w r")

                        dve.tensor_copy(rows_of(1, SMALL), feats_ps[:, 0:SMALL, rs])
                        for p in range(FIELDS):
                            hi = SMALL if p < SMALL else FIELDS
                            chunk = 1 if SMALL <= p < SPLIT else 0
                            row = small_row(p) if p < SMALL else large_row(p)
                            last = dve.tensor_tensor(
                                rows_of(chunk * ROWS + row, hi - p), feats_ps[:, p:hi, rs],
                                feats[:, p:p + 1, rs].broadcast_to([P, hi - p, RH]), ALU.mult)
                        last.then_inc(pairs_made, 1)

        @block.tensor
        def _(pe):
            pe.wait_ge(s1_steps, 2)
            for j in range(FIELDS):
                if j >= 4:
                    pe.wait_ge(u_kept, j - 3)
                for half in range(2):
                    last = pe.matmul(banks[:, 2 * (j % 4) + half, 0:US // 2], w2_sb[:, j, :],
                                     s1[:, half * (US // 2):(half + 1) * (US // 2)], start=True, stop=True)
                last.then_inc(u_made, 1)

            pe.wait_ge(ident_made, 1)
            pe.wait_ge(u_kept, FIELDS)
            pe.wait_ge(wh_steps, 8)
            for k in range(TURNS):
                if k >= 3:
                    pe.wait_ge(bank_drained, k - 2)
                for u in range(4 * k, min(4 * k + 4, UNITS)):
                    last = pe.transpose(banks[0:ROWS, RING[k % 3], (u % 4) * H:(u % 4 + 1) * H],
                                        wh[:, u, :], ident[:, :])
                last.then_inc(bank_filled, 1)
            pe.wait_ge(bank_drained, TURNS)
            pe.wait_ge(top_loaded, 16 * 7)

            with pe.Fori(0, LOOPS) as g:
                for t in range(PER_UNROLL):
                    pe.wait_ge(blocks_made, g * 2 + (t + 1))
                    for k, (c, r0) in enumerate(FILLS):
                        if r0 % RH == 0 and c == 0:
                            pe.wait_ge(pairs_made, g * 4 + (2 * t + HALVES + r0 // RH + 1))
                        pe.wait_ge(bank_drained, fill(g, t, k - 2))
                        width = COLS[c] * Q
                        for r in range(r0, r0 + RPB[c]):
                            at = (r - r0) * width
                            last = pe.matmul(banks[0:ROWS, ring_bank(t, k), at:at + width],
                                             pairs[r // RH][:, r % RH, c * ROWS:(c + 1) * ROWS],
                                             blocks[t][:, r, 0:COLS[c], :].rearrange("p c q -> p (c q)"),
                                             start=True, stop=True)
                        last.then_inc(bank_filled, 1)
                    pe.wait_ge(bank_drained, fill(g, t + 1, 0))
                    for u in Z2_UNITS:
                        mm = pe.matmul(z_ps[:, 1, :], wr[:, u, :], sums[:, u, :],
                                       start=(u == Z2_UNITS[0]), stop=(u == Z2_UNITS[-1]))
                        if u == Z2_UNITS[0]:
                            mm.then_inc(blocks_free[t], 1)
                    for u in UNIT0:
                        pe.matmul(z_ps[:, 0, :], wr[:, u, :], sums[:, u, :], start=(u == 0), stop=False)
                    pe.wait_ge(cross_moved, g * (32 * SMALL) + (16 * SMALL * (t + 1)))
                    pe.matmul(z_ps[:, 0, :], wr[0:CROSS_ROWS, CROSS, :], cross[:, :],
                              start=False, stop=True).then_inc(z_made, 1)
                    pe.wait_ge(z_kept, g * 2 + (t + 1))
                    for m in range(TOP1 // P):
                        ms = slice(m * P, (m + 1) * P)
                        pe.matmul(h1_ps[:, m, :], wt1_z[:, 0, ms], z_sb[:, 0, :], start=True, stop=False)
                        pe.matmul(h1_ps[:, m, :], wt1_z[:, 1, ms], z_sb[:, 1, :], start=False, stop=False)
                        last = pe.matmul(h1_ps[:, m, :], wt1_d[:, ms],
                                         dense_sb[:, bass.ds(g * (2 * P) + t * P, P)], start=False, stop=True)
                    last.then_inc(h1_made, 1)
                    pe.wait_ge(h1_kept, g * 2 + (t + 1))
                    for m in range(TOP2 // P):
                        for c in range(TOP1 // P):
                            last = pe.matmul(h2_ps[:, m, :], wt2_sb[:, c, m * P:(m + 1) * P], h1_sb[:, c, :],
                                             start=(c == 0), stop=(c == TOP1 // P - 1))
                    last.then_inc(h2_made, 1)
                    pe.wait_ge(h2_kept, g * 2 + (t + 1))
                    for c in range(TOP2 // P):
                        last = pe.matmul(y_ps, wt3_sb[:, c:c + 1], h2_sb[:, c, :],
                                         start=(c == 0), stop=(c == TOP2 // P - 1))
                    last.then_inc(y_made, 1)

        @block.scalar
        def _(act):
            for j in range(FIELDS):
                act.wait_ge(u_made, j + 1)
                act.activation(u_mem[:, j * US:(j + 1) * US].rearrange("h (b w) -> h b w", b=2),
                               banks[:, 2 * (j % 4):2 * (j % 4) + 2, 0:US // 2], ACT.Copy).then_inc(u_kept, 1)
            for k in range(TURNS):
                act.wait_ge(bank_filled, k + 1)
                n = min(4, UNITS - 4 * k)
                act.activation(wr[:, 4 * k:4 * k + n, :].rearrange("w u h -> w (u h)"),
                               banks[0:ROWS, RING[k % 3], 0:n * H], ACT.Copy).then_inc(bank_drained, 1)
            act.wait_ge(top_loaded, 16 * 7)
            with act.Fori(0, LOOPS) as g:
                for t in range(PER_UNROLL):
                    for k, (c, r0) in enumerate(FILLS):
                        act.wait_ge(bank_filled, fill(g, t, k + 1))
                        src = banks[0:ROWS, ring_bank(t, k), 0:RPB[c] * COLS[c] * Q].rearrange(
                            "w (r c q) -> w c r q", r=RPB[c], q=Q)
                        act.activation(sums[:, UNIT0[c]:UNIT0[c] + COLS[c], r0 * Q:(r0 + RPB[c]) * Q].rearrange(
                            "w c (r q) -> w c r q", q=Q), src, ACT.Copy).then_inc(bank_drained, 1)
                    act.wait_ge(z_made, g * 2 + (t + 1))
                    for l in range(2):
                        last = act.activation(z_sb[:, l, :], z_ps[:, l, :], ACT.Identity, bias=b12k[:, l:l + 1])
                    last.then_inc(z_kept, 1)
                    act.wait_ge(h1_made, g * 2 + (t + 1))
                    for m in range(TOP1 // P):
                        last = act.activation(h1_sb[:, m, :], h1_ps[:, m, :], ACT.Relu, bias=bt1_sb[:, m:m + 1])
                    last.then_inc(h1_kept, 1)
                    act.wait_ge(h2_made, g * 2 + (t + 1))
                    for m in range(TOP2 // P):
                        last = act.activation(h2_sb[:, m, :], h2_ps[:, m, :], ACT.Relu, bias=bt2_sb[:, m:m + 1])
                    last.then_inc(h2_kept, 1)
                    act.wait_ge(y_made, g * 2 + (t + 1))
                    act.activation(y_sb[:, bass.ds(g * (2 * P) + t * P, P)], y_ps, ACT.Copy).then_inc(y_kept, 1)


def kernel(**inputs):
    import numpy as np
    import concourse.bacc as bacc
    from concourse.bass_utils import run_bass_kernel_spmd as run

    x = {name: np.asarray(a) for name, a in inputs.items()}
    ids = x["ids"].reshape(TILES, R, Q, FIELDS).transpose(0, 2, 1, 3).reshape(BATCH, FIELDS)
    arrays = {"ids": ids}
    for f in range(FIELDS):
        arrays[f"tbl_{f}"] = x[f"tbl_{f}"]
    arrays |= {
        "dense_t": x["dense_ctx"].T,
        "w1": x["L0_rec_W1"].reshape(H, PAIRS),
        "w2_t": x["L0_rec_W2"].transpose(1, 2, 0).reshape(H, FIELDS * H),
        "b1": x["L0_rec_b1"].reshape(H, 1),
        "b2": x["L0_rec_b2"].reshape(H, 1),
        "wt1": x["W_top1"],
        "bt1": x["b_top1"].reshape(TOP1 // P, P).T,
        "wt2": x["W_top2"],
        "bt2": x["b_top2"].reshape(TOP2 // P, P).T,
        "wt3": x["W_top3"].reshape(TOP2 // P, P).T,
    }
    arrays = {name: np.ascontiguousarray(a) for name, a in arrays.items()}
    nc = bacc.Bacc("TRN2", target_bir_lowering=False, num_devices=1)
    aps = {n: nc.dram_tensor(f"in_{n}", a.shape, mybir.dt.from_np(a.dtype), kind="ExternalInput").ap()
           for n, a in arrays.items()}
    out = nc.dram_tensor("out_y", (1, BATCH), F32, kind="ExternalOutput").ap()
    tables = [aps.pop(f"tbl_{f}") for f in range(FIELDS)]
    dlrm_tower(nc, tables=tables, out=out, **aps)
    r = run(nc, [{f"in_{n}": a for n, a in arrays.items()}], core_ids=[0])
    return r.results[0]["out_y"].reshape(BATCH, 1)
```

```python
import concourse.bass as bass
from concourse import mybir
from contextlib import ExitStack

F32 = mybir.dt.float32
I32 = mybir.dt.int32
ALU = mybir.AluOpType
ACT = mybir.ActivationFunctionType

BATCH, FIELDS, K, H = 1024, 26, 32, 128
DENSE, TOP1, TOP2 = 16, 512, 256
P = 128
TILES = BATCH // P
Q = P // K
R = P // Q
HALVES, RH = 2, R // 2

SMALL = 9
SPLIT = 15
LARGE = FIELDS - SMALL
ONE_ROWS = 1 + SMALL


def small_row(a):
    return ONE_ROWS + sum(SMALL - x for x in range(a))


def large_row(p):
    lo, base = (SPLIT, small_row(SMALL)) if p >= SPLIT else (SMALL, 0)
    return base + sum(FIELDS - x for x in range(lo, p))


def pair_rows():
    for p in range(FIELDS):
        if p < SMALL:
            yield p, 0, small_row(p), SMALL
        else:
            yield p, int(p < SPLIT), large_row(p), FIELDS


ROWS = (large_row(FIELDS - 1) + 1, large_row(SPLIT - 1) + FIELDS - SPLIT + 1)
ALL_ROWS = sum(ROWS)
COLS = (1 + FIELDS, 1 + SPLIT)
UNIT0 = (0, COLS[0])
SUM_UNITS = sum(COLS)
CROSS_S = (slice(0, P // LARGE - 2), slice(P // LARGE - 2, SMALL))
CROSS_ROWS = [(c.stop - c.start) * LARGE for c in CROSS_S]
UNITS = SUM_UNITS + len(CROSS_S)
Z2_UNITS = [u for u in range(SUM_UNITS) if u not in UNIT0]

PAIRS = FIELDS * FIELDS
US = PAIRS + 2
BANK = 512
RPB = (4, 8)
EARLY = 14
LOOPS = TILES // 2 - 1
FILLS = [(c, r) for b in range(R // 8) for c, r in ((0, 8 * b), (0, 8 * b + 4), (1, 8 * b))]
TURNS = -(-UNITS // 4)
assert max(ROWS + tuple(CROSS_ROWS)) <= P and TURNS % 3 == 0 == len(FILLS) % 3
assert max(RPB[c] * COLS[c] * Q for c in (0, 1)) <= BANK


WH_DONE = FIELDS + 3


def unit_rows(u):
    if u >= SUM_UNITS:
        return CROSS_ROWS[u - SUM_UNITS]
    return ROWS[int(u >= UNIT0[1])]


def dlrm_tower(nc, ids, tables, dense_t, w1, w2_t, b1, b2, wt1, bt1, wt2, bt2, wt3, out):
    with ExitStack() as ctx:
        def sb(name, shape, dt=F32):
            return ctx.enter_context(nc.sbuf_tensor(name, shape, dt))

        def sem(name):
            return ctx.enter_context(nc.semaphore(name))

        idx = [sb(f"idx{t}", [P, FIELDS], I32) for t in range(2)]
        rows = [sb(f"rows{t}", [P, FIELDS * K]) for t in range(2)]
        feats = sb("feats", [P, FIELDS, R])
        pairs = [sb(f"pairs{h}", [P, RH, ALL_ROWS]) for h in range(HALVES)]
        blocks = [sb(f"blocks{h}", [P, RH, COLS[0], Q]) for h in range(HALVES)]
        sums = sb("sums", [ROWS[0], SUM_UNITS, P])
        s1 = sb("s1", [P, US])
        wh = sb("wh", [P, UNITS, ROWS[0]])
        cross = [sb(f"cross{c}", [n, P]) for c, n in enumerate(CROSS_ROWS)]
        ident = sb("ident", [P, P])
        b12 = sb("b12", [P, 2])
        b12k = sb("b12k", [P, 2])
        z_sb = sb("z_sb", [H, 2, P])
        h1_sb = sb("h1_sb", [P, TOP1 // P, P])
        h2_sb = sb("h2_sb", [P, TOP2 // P, P])
        y_sb = sb("y_sb", [1, BATCH])
        wt3_sb = sb("wt3_sb", [P, TOP2 // P])
        bt1_sb = sb("bt1_sb", [P, TOP1 // P])
        bt2_sb = sb("bt2_sb", [P, TOP2 // P])
        wr_mem = sb("wr_mem", [P, UNITS * H])
        w2_sb = wr_mem[:, 0:FIELDS * H].rearrange("i (j h) -> i j h", j=FIELDS)
        w1_sb = wr_mem[:, FIELDS * H:FIELDS * H + PAIRS].rearrange("i (a b) -> i a b", a=FIELDS)
        wr = wr_mem[:, :].rearrange("w (u h) -> w u h", h=H)
        u_mem = sb("u_mem", [P, FIELDS * US])
        at = [0]

        def after_u(n, words):
            at[0] += words
            return u_mem[0:n, at[0] - words:at[0]]

        wt1_z = after_u(H, 2 * TOP1).rearrange("h (l n) -> h l n", l=2)
        wt1_d = after_u(DENSE, TOP1)
        wt2_sb = after_u(P, TOP1 // P * TOP2).rearrange("h (m n) -> h m n", n=TOP2)
        dense_sb = after_u(DENSE, BATCH)

        banks = ctx.enter_context(nc.psum_tensor("banks", [P, 8, BANK], F32))
        feats_ps = banks[:, 0:2, :].rearrange("p b w -> p (b w)")[:, 0:FIELDS * R].rearrange(
            "p (f r) -> p f r", r=R)
        RING = (2, 3, 4)
        z_ps = banks[:, 5, 0:2 * P].rearrange("h (l n) -> h l n", l=2)
        h1_ps = banks[:, 6, :].rearrange("h (m n) -> h m n", n=P)
        h2_ps = banks[:, 7, 0:TOP2 // P * P].rearrange("h (m n) -> h m n", n=P)
        y_ps = banks[0:1, 7, 3 * P:4 * P]

        w_loaded = sem("w_loaded")
        small_loaded = sem("small_loaded")
        top_loaded = sem("top_loaded")
        ids_loaded = [sem(f"ids_loaded{t}") for t in range(2)]
        rows_gathered = [sem(f"rows_gathered{t}") for t in range(2)]
        gather_started = sem("gather_started")
        ident_zeroed = sem("ident_zeroed")
        ident_made = sem("ident_made")
        s1_steps = sem("s1_steps")
        u_made = sem("u_made")
        u_kept = sem("u_kept")
        zeroed = sem("zeroed")
        wh_steps = sem("wh_steps")
        feats_made = sem("feats_made")
        pairs_made = sem("pairs_made")
        bank_filled = sem("bank_filled")
        bank_drained = sem("bank_drained")
        cross_moved = sem("cross_moved")
        z_made, z_kept = sem("z_made"), sem("z_kept")
        h1_made, h1_kept = sem("h1_made"), sem("h1_kept")
        h2_made, h2_kept = sem("h2_made"), sem("h2_kept")
        y_made, y_kept = sem("y_made"), sem("y_kept")
        out_stored = sem("out_stored")

        LAST = (LOOPS, 1)

        def fill(g, t, k):
            return g * (2 * len(FILLS)) + (TURNS + t * len(FILLS) + k)

        def u_view(j, p, q, outer, inner):
            return bass.AP(u_mem, j * US + p * FIELDS + q, [[FIELDS * US, P], list(outer), list(inner)])

        def wh_view(unit, row, outer, inner):
            return bass.AP(wh, unit * ROWS[0] + row, [[UNITS * ROWS[0], P], list(outer), list(inner)])

        def parts_of_middle(p):
            _, chunk, row, hi = list(pair_rows())[p]
            unit, nz = UNIT0[chunk] + 1, hi - p
            first = (wh_view(unit, row, (ROWS[0], p + 1), (1, nz)), u_view(0, p, p, (US, p + 1), (1, nz)))
            second = p > 0 and (wh_view(unit, row, (ROWS[0], p), (1, nz)),
                                u_view(p, p, 0, (1, p), (FIELDS, nz)))
            third = nz > 1 and (wh_view(unit, row + 1, (ROWS[0], p + 1), (1, nz - 1)),
                                u_view(p + 1, 0, p, (FIELDS, p + 1), (US, nz - 1)))
            return first, second, third

        def parts_of_lowest(a):
            unit, row, ny = 1 + SMALL, small_row(a), SMALL - a
            first = (wh_view(unit, row, (ROWS[0], LARGE), (1, ny)),
                     u_view(a, a, SMALL, (1, LARGE), (FIELDS, ny)))
            second = ny > 1 and (wh_view(unit, row + 1, (ROWS[0], LARGE), (1, ny - 1)),
                                 u_view(a + 1, SMALL, a, (FIELDS, LARGE), (US, ny - 1)))
            third = (wh_view(unit, row, (ROWS[0], LARGE), (1, ny)),
                     u_view(SMALL, a, a, (US, LARGE), (1, ny)))
            return first, second, third

        block = ctx.enter_context(nc.Block())

        @block.sync
        def _(sp):
            sp.dma_start(idx[0][:, :], ids[0:P, :]).then_inc(ids_loaded[0], 16)
            sp.dma_start(w1_sb.rearrange("i a b -> i (a b)"), w1).then_inc(w_loaded, 16)
            sp.dma_start(b12[:, 0:1], b1).then_inc(w_loaded, 16)
            sp.dma_start(b12[:, 1:2], b2).then_inc(w_loaded, 16)
            sp.dma_start(w2_sb.rearrange("i j h -> i (j h)"), w2_t).then_inc(w_loaded, 16)
            sp.dma_start(idx[1][:, :], ids[P:2 * P, :]).then_inc(ids_loaded[1], 16)
            sp.dma_start(wt3_sb[:, :], wt3).then_inc(small_loaded, 16)
            sp.dma_start(bt1_sb[:, :], bt1).then_inc(small_loaded, 16)
            sp.dma_start(bt2_sb[:, :], bt2).then_inc(small_loaded, 16)

            def load_ids(g, t):
                sp.wait_ge(feats_made, g * 2 + t)
                sp.dma_start(idx[(t + 1) % 2][:, :],
                             ids[bass.ds(g * (2 * P) + (t + 1) * P, P), :]).then_inc(ids_loaded[(t + 1) % 2], 16)

            sp.wait_ge(feats_made, 1)
            sp.dma_start(idx[0][:, :], ids[2 * P:3 * P, :]).then_inc(ids_loaded[0], 16)
            sp.wait_ge(wh_steps, WH_DONE)
            sp.dma_start(wt1_z, wt1[0:2 * H, :].rearrange("(l h) n -> h l n", l=2)).then_inc(top_loaded, 16)
            sp.dma_start(wt1_d, wt1[2 * H:2 * H + DENSE, :]).then_inc(top_loaded, 16)
            sp.dma_start(dense_sb, dense_t).then_inc(top_loaded, 16)
            sp.dma_start(wt2_sb, wt2.rearrange("(m h) n -> h m n", h=P)).then_inc(top_loaded, 16)
            load_ids(0, 2)
            with sp.Fori(1, LOOPS) as g:
                for t in (1, 2):
                    load_ids(g, t)
            sp.wait_ge(y_kept, TILES)
            sp.dma_start(out, y_sb[:, :]).then_inc(out_stored, 16)
            sp.wait_ge(out_stored, 16)

        @block.gpsimd
        def _(pool):
            pool.memset(ident[:, :], 0.0).then_inc(ident_zeroed, 1)
            pool.wait_ge(ident_zeroed, 1)
            pool.affine_select(out=ident[:, :], in_=ident[:, :], compare_op=ALU.not_equal, fill=1.0,
                               base=0, pattern=[[-1, P]], channel_multiplier=1).then_inc(ident_made, 1)
            with pool.Fori(0, TILES // 2) as g:
                for t in range(2):
                    pool.wait_ge(ids_loaded[t], (g + 1) * 16)
                    pool.sem_inc(gather_started, 1)
                    for f in range(FIELDS):
                        pool.indirect_dma_start(
                            rows[t][:, f * K:(f + 1) * K], None, tables[f],
                            bass.IndirectOffsetOnAxis(ap=idx[t][:, f:f + 1], axis=0),
                        ).then_inc(rows_gathered[t], 16)

        @block.vector
        def _(dve):
            dve.memset(wh[:, :, :].rearrange("h u w -> h (u w)"), 0.0)
            for h in range(HALVES):
                last = dve.memset(blocks[h][:, :, :, :].rearrange("p r c q -> p (r c q)"), 0.0)
            last.then_inc(zeroed, 1)
            dve.memset(s1[:, PAIRS + 1:US], 0.0)
            dve.wait_ge(w_loaded, 64)
            s1_ab = s1[:, 0:PAIRS].rearrange("i (a b) -> i a b", a=FIELDS)
            dve.tensor_tensor(s1_ab, w1_sb, w1_sb.rearrange("i a b -> i b a"), ALU.add).then_inc(s1_steps, 1)
            dve.tensor_copy(s1[:, PAIRS:PAIRS + 1], b12[:, 0:1])
            dve.wait_ge(s1_steps, 1)
            dve.tensor_copy(s1[:, 0:PAIRS:FIELDS + 1],
                            w1_sb.rearrange("i a b -> i (a b)")[:, 0:PAIRS:FIELDS + 1]).then_inc(s1_steps, 1)
            dve.tensor_scalar(b12k[:, :], b12[:, :], float(K), None, ALU.mult)
            dve.wait_ge(zeroed, 1)
            for h in range(HALVES):
                for q in range(Q):
                    dve.memset(blocks[h][q * K:(q + 1) * K, :, 0, q], 1.0)
                dve.memset(pairs[h][:, :, 0], 1.0)
            dve.wait_ge(s1_steps, 2)
            for p, chunk, row, hi in pair_rows():
                dve.tensor_copy(wh[:, UNIT0[chunk], row:row + hi - p], s1_ab[:, p, p:hi])
            for c, ss in enumerate(CROSS_S):
                dve.tensor_copy(wh[:, SUM_UNITS + c, 0:CROSS_ROWS[c]].rearrange("h (s q) -> h s q", q=LARGE),
                                s1_ab[:, ss, SMALL:FIELDS])

            def first_two(p):
                first, second, _ = parts_of_middle(p)
                dve.wait_ge(u_kept, p + 1)
                dve.tensor_copy(*first).then_inc(wh_steps, 1)
                if second:
                    dve.wait_ge(wh_steps, p + 1)
                    dve.tensor_tensor(second[0], second[0], second[1], ALU.add)

            def tile(g, t, first=False):
                dve.wait_ge(rows_gathered[t % 2], (g + (t // 2 + 1)) * (16 * FIELDS))
                if not first:
                    dve.wait_ge(pairs_made, g * 4 + HALVES * t)
                dve.transpose(feats[:, :, :].rearrange("p f r -> p (f r)"), rows[t % 2][:, :])
                dve.transpose(feats_ps.rearrange("p f r -> p (f r)"), rows[t % 2][:, :]).then_inc(feats_made, 1)
                dve.wait_ge(feats_made, g * 2 + (t + 1))
                for h in range(HALVES):
                    if not first:
                        dve.wait_ge(bank_filled, fill(g, t - 1, (h + 1) * len(FILLS) // HALVES))
                    rs = slice(h * RH, (h + 1) * RH)
                    for q in range(Q):
                        part = slice(q * K, (q + 1) * K)
                        dve.tensor_copy(blocks[h][part, :, 1:COLS[0], q].rearrange("p r f -> p f r"),
                                        feats_ps[part, :, rs])

                    def to_rows(row, n):
                        return pairs[h][:, :, row:row + n].rearrange("p r w -> p w r")

                    dve.tensor_copy(to_rows(1, SMALL), feats_ps[:, 0:SMALL, rs])
                    for p, chunk, row, hi in pair_rows():
                        last = dve.tensor_tensor(
                            to_rows(chunk * ROWS[0] + row, hi - p), feats_ps[:, p:hi, rs],
                            feats[:, p:p + 1, rs].broadcast_to([P, hi - p, RH]), ALU.mult)
                    last.then_inc(pairs_made, 1)

            for p in range(EARLY):
                first_two(p)
            tile(0, 0, first=True)
            for p in range(EARLY, FIELDS):
                first_two(p)
            dve.tensor_copy(wh_view(1, 0, (ROWS[0], FIELDS), (1, 1)), u_view(0, 0, PAIRS, (US, FIELDS), (1, 1)))
            for a in range(SMALL):
                last = dve.tensor_copy(*parts_of_lowest(a)[0])
            last.then_inc(wh_steps, 1)
            dve.wait_ge(wh_steps, FIELDS + 1)
            for a in range(SMALL - 1):
                to, second = parts_of_lowest(a)[1]
                last = dve.tensor_tensor(to, to, second, ALU.add)
            last.then_inc(wh_steps, 1)
            dve.wait_ge(wh_steps, FIELDS + 2)
            for parts in [*map(parts_of_middle, range(FIELDS)), *map(parts_of_lowest, range(SMALL))]:
                if parts[2]:
                    to, third = parts[2]
                    last = dve.tensor_tensor(to, to, third, ALU.add)
            last.then_inc(wh_steps, 1)

            with dve.Fori(0, LOOPS) as g:
                for t in (1, 2):
                    tile(g, t)
            tile(*LAST)

        @block.tensor
        def _(pe):
            pe.wait_ge(s1_steps, 2)
            for j in range(FIELDS):
                if j >= 3:
                    pe.wait_ge(u_kept, j - 2)
                for half in range(2):
                    last = pe.matmul(banks[:, 2 + 2 * (j % 3) + half, 0:US // 2], w2_sb[:, j, :],
                                     s1[:, half * (US // 2):(half + 1) * (US // 2)], start=True, stop=True)
                last.then_inc(u_made, 1)

            def sums_fill(g, t, k, first=False):
                c, r0 = FILLS[k]
                if c == 0 and r0 % RH == 0:
                    pe.wait_ge(pairs_made, g * 4 + (2 * t + r0 // RH + 1))
                if not first:
                    pe.wait_ge(bank_drained, fill(g, t, k - 2))
                elif k >= 3:
                    pe.wait_ge(bank_drained, k - 2)
                width = COLS[c] * Q
                for r in range(r0, r0 + RPB[c]):
                    h, at_row = r // RH, c * ROWS[0]
                    last = pe.matmul(banks[0:ROWS[c], RING[k % 3], (r - r0) * width:(r - r0 + 1) * width],
                                     pairs[h][:, r % RH, at_row:at_row + ROWS[c]],
                                     blocks[h][:, r % RH, 0:COLS[c], :].rearrange("p c q -> p (c q)"),
                                     start=True, stop=True)
                last.then_inc(bank_filled, 1)

            def z2(g, t, first=False):
                pe.wait_ge(bank_drained, len(FILLS) + TURNS if first else fill(g, t + 1, 0))
                for u in Z2_UNITS:
                    n = unit_rows(u)
                    pe.matmul(z_ps[:, 1, :], wr[0:n, u, :], sums[0:n, u, :],
                              start=(u == Z2_UNITS[0]), stop=(u == Z2_UNITS[-1]))

            def z1(g, t):
                for c, u in enumerate(UNIT0):
                    pe.matmul(z_ps[:, 0, :], wr[0:ROWS[c], u, :], sums[0:ROWS[c], u, :],
                              start=(c == 0), stop=False)
                pe.wait_ge(cross_moved, g * (32 * SMALL) + 16 * SMALL * (t + 1))
                for c, n in enumerate(CROSS_ROWS):
                    last = pe.matmul(z_ps[:, 0, :], wr[0:n, SUM_UNITS + c, :], cross[c][:, :],
                                     start=False, stop=(c == len(CROSS_ROWS) - 1))
                last.then_inc(z_made, 1)

            def hidden1(g, t):
                pe.wait_ge(z_kept, g * 2 + (t + 1))
                for m in range(TOP1 // P):
                    ms = slice(m * P, (m + 1) * P)
                    pe.matmul(h1_ps[:, m, :], wt1_z[:, 0, ms], z_sb[:, 0, :], start=True, stop=False)
                    pe.matmul(h1_ps[:, m, :], wt1_z[:, 1, ms], z_sb[:, 1, :], start=False, stop=False)
                    last = pe.matmul(h1_ps[:, m, :], wt1_d[:, ms],
                                     dense_sb[:, bass.ds(g * (2 * P) + t * P, P)], start=False, stop=True)
                last.then_inc(h1_made, 1)

            def hidden2(g, t):
                pe.wait_ge(h1_kept, g * 2 + (t + 1))
                for m in range(TOP2 // P):
                    for c in range(TOP1 // P):
                        last = pe.matmul(h2_ps[:, m, :], wt2_sb[:, c, m * P:(m + 1) * P], h1_sb[:, c, :],
                                         start=(c == 0), stop=(c == TOP1 // P - 1))
                last.then_inc(h2_made, 1)

            def output(g, t):
                pe.wait_ge(h2_kept, g * 2 + (t + 1))
                for c in range(TOP2 // P):
                    last = pe.matmul(y_ps, wt3_sb[:, c:c + 1], h2_sb[:, c, :],
                                     start=(c == 0), stop=(c == TOP2 // P - 1))
                last.then_inc(y_made, 1)

            def tile(g, t):
                for k in range(len(FILLS)):
                    sums_fill(g, t, k)
                    if k == 2:
                        hidden1(g, t - 1)
                hidden2(g, t - 1)
                z2(g, t)
                output(g, t - 1)
                z1(g, t)

            pe.wait_ge(u_kept, FIELDS)
            for k in range(len(FILLS)):
                sums_fill(0, 0, k, first=True)
            pe.wait_ge(ident_made, 1)
            pe.wait_ge(wh_steps, WH_DONE)
            for k in range(TURNS):
                pe.wait_ge(bank_drained, len(FILLS) + k - 2)
                for u in range(4 * k, min(4 * k + 4, UNITS)):
                    last = pe.transpose(banks[0:ROWS[0], RING[k % 3], (u % 4) * H:(u % 4 + 1) * H],
                                        wh[:, u, :], ident[:, :])
                last.then_inc(bank_filled, 1)
            z2(0, 0, first=True)
            z1(0, 0)
            pe.wait_ge(top_loaded, 16 * 4)
            pe.wait_ge(small_loaded, 16 * 3)
            with pe.Fori(0, LOOPS) as g:
                for t in (1, 2):
                    tile(g, t)
            tile(*LAST)
            hidden1(*LAST)
            hidden2(*LAST)
            output(*LAST)

        @block.scalar
        def _(act):
            for j in range(FIELDS):
                act.wait_ge(u_made, j + 1)
                act.activation(u_mem[:, j * US:(j + 1) * US].rearrange("h (b w) -> h b w", b=2),
                               banks[:, 2 + 2 * (j % 3):4 + 2 * (j % 3), 0:US // 2], ACT.Copy).then_inc(u_kept, 1)

            def drain(g, t, k, first=False):
                c, r0 = FILLS[k]
                act.wait_ge(bank_filled, k + 1 if first else fill(g, t, k + 1))
                act.activation(
                    sums[0:ROWS[c], UNIT0[c]:UNIT0[c] + COLS[c], r0 * Q:(r0 + RPB[c]) * Q].rearrange(
                        "w c (r q) -> w c r q", q=Q),
                    banks[0:ROWS[c], RING[k % 3], 0:RPB[c] * COLS[c] * Q].rearrange(
                        "w (r c q) -> w c r q", r=RPB[c], q=Q), ACT.Copy).then_inc(bank_drained, 1)

            def move_cross(g, t, first=False):
                act.wait_ge(bank_drained, len(FILLS) if first else fill(g, t + 1, 0))
                for c, ss in enumerate(CROSS_S):
                    for s in range(ss.start, ss.stop):
                        at_row = (s - ss.start) * LARGE
                        act.dma_start(cross[c][at_row:at_row + LARGE, :],
                                      sums[1 + s:2 + s, 1 + SMALL:1 + FIELDS, :]).then_inc(cross_moved, 16)

            def keep_z(g, t):
                act.wait_ge(z_made, g * 2 + (t + 1))
                for l in range(2):
                    last = act.activation(z_sb[:, l, :], z_ps[:, l, :], ACT.Identity, bias=b12k[:, l:l + 1])
                last.then_inc(z_kept, 1)

            def keep_h1(g, t):
                act.wait_ge(h1_made, g * 2 + (t + 1))
                for m in range(TOP1 // P):
                    last = act.activation(h1_sb[:, m, :], h1_ps[:, m, :], ACT.Relu, bias=bt1_sb[:, m:m + 1])
                last.then_inc(h1_kept, 1)

            def keep_h2(g, t):
                act.wait_ge(h2_made, g * 2 + (t + 1))
                for m in range(TOP2 // P):
                    last = act.activation(h2_sb[:, m, :], h2_ps[:, m, :], ACT.Relu, bias=bt2_sb[:, m:m + 1])
                last.then_inc(h2_kept, 1)

            def keep_y(g, t):
                act.wait_ge(y_made, g * 2 + (t + 1))
                act.activation(y_sb[:, bass.ds(g * (2 * P) + t * P, P)], y_ps, ACT.Copy).then_inc(y_kept, 1)

            def tile(g, t):
                keep_z(g, t - 1)
                for k in range(len(FILLS)):
                    drain(g, t, k)
                    if k == 2:
                        keep_h1(g, t - 1)
                move_cross(g, t)
                keep_h2(g, t - 1)
                keep_y(g, t - 1)

            for k in range(len(FILLS)):
                drain(0, 0, k, first=True)
            move_cross(0, 0, first=True)
            for k in range(TURNS):
                act.wait_ge(bank_filled, len(FILLS) + k + 1)
                n = min(4, UNITS - 4 * k)
                act.activation(wr[0:ROWS[0], 4 * k:4 * k + n, :].rearrange("w u h -> w (u h)"),
                               banks[0:ROWS[0], RING[k % 3], 0:n * H], ACT.Copy).then_inc(bank_drained, 1)
            act.wait_ge(small_loaded, 16 * 3)
            with act.Fori(0, LOOPS) as g:
                for t in (1, 2):
                    tile(g, t)
            tile(*LAST)
            keep_z(*LAST)
            keep_h1(*LAST)
            keep_h2(*LAST)
            keep_y(*LAST)


def kernel(**inputs):
    import numpy as np
    import concourse.bacc as bacc
    from concourse.bass_utils import run_bass_kernel_spmd as run

    x = {name: np.asarray(a) for name, a in inputs.items()}
    ids = x["ids"].reshape(TILES, R, Q, FIELDS).transpose(0, 2, 1, 3).reshape(BATCH, FIELDS)
    arrays = {"ids": ids}
    for f in range(FIELDS):
        arrays[f"tbl_{f}"] = x[f"tbl_{f}"]
    arrays |= {
        "dense_t": x["dense_ctx"].T,
        "w1": x["L0_rec_W1"].reshape(H, PAIRS),
        "w2_t": x["L0_rec_W2"].transpose(1, 2, 0).reshape(H, FIELDS * H),
        "b1": x["L0_rec_b1"].reshape(H, 1),
        "b2": x["L0_rec_b2"].reshape(H, 1),
        "wt1": x["W_top1"],
        "bt1": x["b_top1"].reshape(TOP1 // P, P).T,
        "wt2": x["W_top2"],
        "bt2": x["b_top2"].reshape(TOP2 // P, P).T,
        "wt3": x["W_top3"].reshape(TOP2 // P, P).T,
    }
    arrays = {name: np.ascontiguousarray(a) for name, a in arrays.items()}
    nc = bacc.Bacc("TRN2", target_bir_lowering=False, num_devices=1)
    aps = {n: nc.dram_tensor(f"in_{n}", a.shape, mybir.dt.from_np(a.dtype), kind="ExternalInput").ap()
           for n, a in arrays.items()}
    out = nc.dram_tensor("out_y", (1, BATCH), F32, kind="ExternalOutput").ap()
    tables = [aps.pop(f"tbl_{f}") for f in range(FIELDS)]
    dlrm_tower(nc, tables=tables, out=out, **aps)
    r = run(nc, [{f"in_{n}": a for n, a in arrays.items()}], core_ids=[0])
    return r.results[0]["out_y"].reshape(BATCH, 1)
```

```python
import concourse.bass as bass
from concourse import mybir
from contextlib import ExitStack

F32 = mybir.dt.float32
I32 = mybir.dt.int32
ALU = mybir.AluOpType
ACT = mybir.ActivationFunctionType

BATCH, FIELDS, K, H = 1024, 26, 32, 128
DENSE, TOP1, TOP2 = 16, 512, 256
P = 128
TILES = BATCH // P
Q = P // K
R = P // Q
HALVES, RH = 2, R // 2

MID0, HIGH0 = 9, 15
LAST0 = 4
MIDS, HIGHS = HIGH0 - MID0, FIELDS - HIGH0
GROUPS = (range(HIGH0, FIELDS), range(MID0, HIGH0), range(LAST0, MID0), range(LAST0))
HOT = (0, 3)
HOT0 = 3
HOT_N = (TILES - HOT0) * R
HOT_CHUNKS = 8
GATHERED = [f for f in GROUPS[-1] if f not in HOT]
assert HOT0 % 2 and GATHERED == list(range(GATHERED[0], GATHERED[-1] + 1)) and len(HOT) <= 2


def triangle(n, first=0):
    return sum(n - a for a in range(first, n))


SMALL_PAIRS = 1 + MID0
HIGH_PAIRS = SMALL_PAIRS + triangle(MID0)
RECT = HIGH_PAIRS + triangle(FIELDS, HIGH0)
MID_PAIRS = RECT + HIGH0 * HIGHS
CORNER = MID_PAIRS + triangle(HIGH0, MID0)
US = CORNER + MID0 * MIDS


def small_at(a):
    return SMALL_PAIRS + sum(MID0 - x for x in range(a))


def mid_at(a):
    return MID_PAIRS + sum(HIGH0 - x for x in range(MID0, a))


def high_at(a):
    return HIGH_PAIRS + sum(FIELDS - x for x in range(HIGH0, a))


def rect_at(x, z):
    return RECT + x * HIGHS + z - HIGH0


def corner_at(s, m):
    return CORNER + s * MIDS + m - MID0


TRIANGLES = ([(a, small_at(a), MID0) for a in range(MID0)]
             + [(a, mid_at(a), HIGH0) for a in range(MID0, HIGH0)]
             + [(a, high_at(a), FIELDS) for a in range(HIGH0, FIELDS)])

ROW0 = (0, rect_at(MID0, HIGH0))
ROWS = (RECT, CORNER - ROW0[1])
ALL_ROWS = sum(ROWS)
COLS = (1 + FIELDS, 1 + HIGH0)
UNIT0 = (0, COLS[0])
SUM_UNITS = sum(COLS)
CROSS_UNIT = SUM_UNITS
CROSS_ROWS = MID0 * HIGHS
CORNER_S = (P - ROWS[1]) // MIDS
REST_UNIT = CROSS_UNIT + 1
REST_ROWS = (MID0 - CORNER_S) * MIDS
UNITS = REST_UNIT + 1
ONES_ROWS = ROWS[1] + CORNER_S * MIDS
SPARE = P - ROWS[1]
PACKED = 4
KEPT = HIGH0 - PACKED
PIECES = ROWS[1] // SPARE
LEFT = ROWS[1] - PIECES * SPARE
assert PACKED * PIECES < KEPT and PACKED * LEFT <= SPARE and CROSS_ROWS + REST_ROWS <= P


def z2_rows(unit):
    if unit < UNIT0[1]:
        return ROWS[0]
    x = unit - UNIT0[1] - 1
    if x < PACKED * PIECES:
        return P
    return ROWS[1] + (PACKED * LEFT if x == PACKED * PIECES else 0) if x < KEPT else 0


Z2_UNITS = [[u for u in range(UNIT0[c] + 1, UNIT0[c] + COLS[c]) if z2_rows(u)] for c in (0, 1)]

PAIRS = FIELDS * FIELDS
BANK = 512
RPB = (4, 8)
LOOPS = TILES // 2 - 1
FILLS = [(c, r) for b in range(R // 8) for c, r in ((0, 8 * b), (0, 8 * b + 4), (1, 8 * b))]
TURNS = -(-UNITS // 4)
assert max(ROWS) <= P and TURNS % 3 == 0 == len(FILLS) % 3
assert max(RPB[c] * COLS[c] * Q for c in (0, 1)) <= BANK and US <= BANK


def weights_of(u):
    if u == CROSS_UNIT:
        return None, RECT, CROSS_ROWS
    if u == REST_UNIT:
        return None, US - REST_ROWS, REST_ROWS
    if u == UNIT0[1]:
        return None, ROW0[1], ONES_ROWS
    c = int(u >= UNIT0[1])
    return (None if u in UNIT0 else u - UNIT0[c] - 1), ROW0[c], ROWS[c]


def dlrm_tower(nc, ids, hot_ids, table_row, tables, dense_t, w1, w2_t, b1, b2, wt1, bt1, wt2, bt2, wt3, out):
    with ExitStack() as ctx:
        def sb(name, shape, dt=F32):
            return ctx.enter_context(nc.sbuf_tensor(name, shape, dt))

        def sem(name):
            return ctx.enter_context(nc.semaphore(name))

        idx = [sb(f"idx{t}", [P, FIELDS], I32) for t in range(2)]
        rows = [sb(f"rows{t}", [P, FIELDS * K]) for t in range(2)]
        feats = sb("feats", [P, FIELDS, R])
        pairs = [sb(f"pairs{h}", [P, RH, ALL_ROWS]) for h in range(HALVES)]
        blocks = [sb(f"blocks{h}", [P, RH, COLS[0], Q]) for h in range(HALVES)]
        sums = sb("sums", [P, SUM_UNITS, P])
        s1 = sb("s1", [P, US])
        u_mem = sb("u_mem", [P, FIELDS, US])
        cross = sb("cross", [CROSS_ROWS + REST_ROWS, P])
        ident = sb("ident", [P, P])
        hot_idx = sb("hot_idx", [P, len(HOT), Q * HOT_N], I32)
        row_sb = sb("row_sb", [P, HOT_CHUNKS])
        hot_tables = [sb(f"hot_table{f}", [tables[f].shape[0] // HOT_CHUNKS, HOT_CHUNKS, K]) for f in HOT]
        one_hot = sb("one_hot", [P, HOT_CHUNKS, Q * HOT_N])
        hot_feats = sb("hot_feats", [P, len(HOT), HOT_N])
        b12 = sb("b12", [P, 2])
        b2k = sb("b2k", [P, 1])
        z_sb = sb("z_sb", [H, 2, P])
        h1_sb = sb("h1_sb", [P, TOP1 // P, P])
        h1_dense = sb("h1_dense", [P, TOP1 // P, BATCH])
        h2_sb = sb("h2_sb", [P, TOP2 // P, P])
        y_sb = sb("y_sb", [1, BATCH])
        wt1_z = sb("wt1_z", [H, 2, TOP1])
        wt1_d = sb("wt1_d", [P, TOP1])
        wt2_sb = sb("wt2_sb", [P, TOP1 // P, TOP2])
        wt3_sb = sb("wt3_sb", [P, TOP2 // P])
        bt1_sb = sb("bt1_sb", [P, TOP1 // P])
        bt2_sb = sb("bt2_sb", [P, TOP2 // P])
        dense_sb = sb("dense_sb", [P, BATCH])
        wr_mem = sb("wr_mem", [P, UNITS * H])
        w2_sb = wr_mem[:, 0:FIELDS * H].rearrange("i (j h) -> i j h", j=FIELDS)
        w1_sb = wr_mem[:, FIELDS * H:FIELDS * H + PAIRS].rearrange("i (a b) -> i a b", a=FIELDS)
        wr = wr_mem[:, :].rearrange("w (u h) -> w u h", h=H)

        banks = ctx.enter_context(nc.psum_tensor("banks", [P, 8, BANK], F32))
        feats_ps = banks[:, 0:2, :].rearrange("p b w -> p (b w)")[:, 0:FIELDS * R].rearrange(
            "p (f r) -> p f r", r=R)
        RING = (2, 3, 4)
        U_RING = (2, 3, 4, 5, 6, 7)
        z_ps = banks[:, 5, 0:2 * P].rearrange("h (l n) -> h l n", l=2)
        h1_ps = banks[:, 6, :].rearrange("h (m n) -> h m n", n=P)
        h2_ps = banks[:, 7, 0:TOP2 // P * P].rearrange("h (m n) -> h m n", n=P)
        y_ps = banks[0:1, 7, 3 * P:4 * P]
        DENSE_BANKS = (5, 6, 7)
        HOT_BANKS = (2, 7)
        DENSE_PARTS = [(m, b) for m in range(TOP1 // P) for b in range(BATCH // BANK)]
        Z1_BANK, H1_BANKS, H2_BANKS = 0, (2, 3, 4, 6), (7, 1)

        w1_loaded = sem("w1_loaded")
        w2_loaded = [sem(f"w2_loaded{k}") for k in range(2)]
        small_loaded = sem("small_loaded")
        top_loaded = sem("top_loaded")
        ids_loaded = [sem(f"ids_loaded{t}") for t in range(2)]
        gathered = [[sem(f"gathered{t}_{n}") for n in range(len(GROUPS))] for t in range(2)]
        gather_started = sem("gather_started")
        ident_zeroed = sem("ident_zeroed")
        ident_made = sem("ident_made")
        s1_steps = sem("s1_steps")
        u_made = sem("u_made")
        u_kept = sem("u_kept")
        dense_zeroed = sem("dense_zeroed")
        zeroed = sem("zeroed")
        folds = sem("folds")
        hot_loaded = sem("hot_loaded")
        hot_ready = sem("hot_ready")
        hot_made, hot_kept = sem("hot_made"), sem("hot_kept")
        late_gathered = [sem(f"late_gathered{t}") for t in range(2)]
        feats_made = [sem(f"feats_made{n}") for n in range(len(GROUPS))]
        upper_made, all_made = feats_made[1], feats_made[-1]
        blocks_made = sem("blocks_made")
        pairs_made = sem("pairs_made")
        bank_filled = sem("bank_filled")
        bank_drained = sem("bank_drained")
        weights_moved = sem("weights_moved")
        cross_moved = sem("cross_moved")
        sums_packed = sem("sums_packed")
        dense_made, dense_kept = sem("dense_made"), sem("dense_kept")
        h1_added = sem("h1_added")
        z_made, z_kept = sem("z_made"), sem("z_kept")
        h1_made, h1_kept = sem("h1_made"), sem("h1_kept")
        h2_made, h2_kept = sem("h2_made"), sem("h2_kept")
        y_made, y_kept = sem("y_made"), sem("y_kept")
        last_z1_made, last_z1_kept = sem("last_z1_made"), sem("last_z1_kept")
        last_h1_made = sem("last_h1_made")
        last_h1_kept = [sem(f"last_h1_kept{m}") for m in range(TOP1 // P)]
        last_h2_made = sem("last_h2_made")
        last_h2_kept = [sem(f"last_h2_kept{m}") for m in range(TOP2 // P)]
        out_stored = sem("out_stored")

        LAST = (LOOPS, 1)

        def fill(g, t, k):
            return g * (2 * len(FILLS)) + (TURNS + t * len(FILLS) + k)

        def u(j, pair, *dims):
            return bass.AP(u_mem, j * US + pair, [[FIELDS * US, P], *map(list, dims)])

        block = ctx.enter_context(nc.Block())

        @block.sync
        def _(sp):
            sp.dma_start(idx[0][:, :], ids[0:P, :]).then_inc(ids_loaded[0], 16)
            sp.dma_start(w1_sb.rearrange("i a b -> i (a b)"), w1).then_inc(w1_loaded, 16)
            sp.dma_start(b12[:, 0:1], b1).then_inc(w1_loaded, 16)
            sp.dma_start(b12[:, 1:2], b2).then_inc(w1_loaded, 16)
            sp.dma_start(row_sb[:, :], table_row).then_inc(hot_loaded, 16)
            sp.dma_start(hot_idx[:, 0, :], hot_ids[0:1, :].broadcast_to([P, Q * HOT_N])).then_inc(hot_loaded, 16)
            for k in range(2):
                js = slice(k * FIELDS // 2, (k + 1) * FIELDS // 2)
                sp.dma_start(w2_sb[:, js, :].rearrange("i j h -> i (j h)"),
                             w2_t[:, js.start * H:js.stop * H]).then_inc(w2_loaded[k], 16)
            sp.dma_start(idx[1][:, :], ids[P:2 * P, :]).then_inc(ids_loaded[1], 16)
            sp.dma_start(wt3_sb[:, :], wt3).then_inc(small_loaded, 16)
            sp.dma_start(bt1_sb[:, :], bt1).then_inc(small_loaded, 16)
            sp.dma_start(bt2_sb[:, :], bt2).then_inc(small_loaded, 16)
            sp.dma_start(wt1_z[:, :, :], wt1[0:2 * H, :].rearrange("(l h) n -> h l n", l=2)).then_inc(top_loaded, 16)
            for i in range(1, len(HOT)):
                sp.dma_start(hot_idx[:, i, :], hot_ids[i:i + 1, :].broadcast_to([P, Q * HOT_N])).then_inc(hot_loaded, 16)
            for i, f in enumerate(HOT):
                sp.dma_start(hot_tables[i][:, :, :],
                             tables[f].rearrange("(p c) k -> p c k", c=HOT_CHUNKS)).then_inc(hot_loaded, 16)
            sp.wait_ge(dense_zeroed, 1)
            sp.dma_start(wt1_d[0:DENSE, :], wt1[2 * H:2 * H + DENSE, :]).then_inc(top_loaded, 16)
            sp.dma_start(dense_sb[0:DENSE, :], dense_t).then_inc(top_loaded, 16)
            sp.dma_start(wt2_sb[:, :, :], wt2.rearrange("(m h) n -> h m n", h=P)).then_inc(top_loaded, 16)

            def load_ids(g, t):
                sp.wait_ge(all_made, g * 2 + (t + 1))
                sp.dma_start(idx[t % 2][:, :],
                             ids[bass.ds(g * (2 * P) + (t + 2) * P, P), :]).then_inc(ids_loaded[t % 2], 16)

            def pack(units, moved):
                hosts = UNIT0[1] + 1
                packed = units[:, hosts + KEPT:hosts + HIGH0, :]
                for n in range(PIECES):
                    sp.dma_start(units[ROWS[1]:P, hosts + n * PACKED:hosts + (n + 1) * PACKED, :],
                                 packed[n * SPARE:(n + 1) * SPARE, :, :]).then_inc(moved, 16)
                sp.dma_start(units[ROWS[1]:ROWS[1] + LEFT * PACKED, hosts + PIECES * PACKED, :],
                             packed[PIECES * SPARE:ROWS[1], :, :]).then_inc(moved, 16)

            def move_sums(g, t):
                sp.wait_ge(bank_drained, fill(g, t + 1, 0))
                pack(sums, sums_packed)
                for to, ss, fs in ((sums[ROWS[1]:ONES_ROWS, UNIT0[1], :], range(CORNER_S), range(MID0, HIGH0)),
                                   (cross[0:CROSS_ROWS, :], range(MID0), range(HIGH0, FIELDS)),
                                   (cross[CROSS_ROWS:CROSS_ROWS + REST_ROWS, :], range(CORNER_S, MID0),
                                    range(MID0, HIGH0))):
                    sp.dma_start(to, sums[1 + ss.start:1 + ss.stop, 1 + fs.start:1 + fs.stop, :]).then_inc(
                        cross_moved, 16)

            sp.wait_ge(bank_drained, TURNS)
            pack(wr, weights_moved)
            sp.dma_start(wr[CROSS_ROWS:CROSS_ROWS + REST_ROWS, CROSS_UNIT, :],
                         wr[0:REST_ROWS, REST_UNIT, :]).then_inc(weights_moved, 16)
            sp.wait_ge(all_made, 1)
            sp.dma_start(idx[0][:, :], ids[2 * P:3 * P, :]).then_inc(ids_loaded[0], 16)
            move_sums(0, 0)
            load_ids(0, 1)
            move_sums(0, 1)
            with sp.Fori(1, LOOPS) as g:
                for t in range(2):
                    load_ids(g, t)
                    move_sums(g, t)
            move_sums(LOOPS, 0)
            move_sums(LOOPS, 1)
            sp.wait_ge(y_kept, TILES)
            sp.dma_start(out, y_sb[:, :]).then_inc(out_stored, 16)
            sp.wait_ge(out_stored, 16)

        @block.gpsimd
        def _(pool):
            pool.memset(ident[:, :], 0.0).then_inc(ident_zeroed, 1)
            pool.wait_ge(ident_zeroed, 1)
            pool.affine_select(out=ident[:, :], in_=ident[:, :], compare_op=ALU.not_equal, fill=1.0,
                               base=0, pattern=[[-1, P]], channel_multiplier=1).then_inc(ident_made, 1)

            def gather(g, t, late=False):
                pool.wait_ge(ids_loaded[t % 2], (g + (t // 2 + 1)) * 16)
                pool.sem_inc(gather_started, 1)
                for n, fs in enumerate(GROUPS):
                    done = gathered[t % 2][n]
                    if late and n == len(GROUPS) - 1:
                        fs, done = GATHERED, late_gathered[t % 2]
                    for f in fs:
                        pool.indirect_dma_start(
                            rows[t % 2][:, f * K:(f + 1) * K], None, tables[f],
                            bass.IndirectOffsetOnAxis(ap=idx[t % 2][:, f:f + 1], axis=0),
                        ).then_inc(done, 16)

            for t in range(HOT0):
                gather(0, t)
            with pool.Fori(HOT0 // 2, LOOPS) as g:
                for t in (1, 2):
                    gather(g, t, late=True)
            gather(*LAST, late=True)

        @block.vector
        def _(dve):
            dve.memset(wt1_d[:, :], 0.0)
            dve.memset(dense_sb[:, :], 0.0).then_inc(dense_zeroed, 1)
            dve.memset(s1[:, 1:SMALL_PAIRS], 0.0)
            dve.wait_ge(w1_loaded, 48)
            diagonal = w1_sb.rearrange("i a b -> i (a b)")[:, 0:PAIRS:FIELDS + 1]
            dve.tensor_scalar(diagonal, diagonal, 0.5, None, ALU.mult).then_inc(s1_steps, 1)
            dve.tensor_copy(s1[:, 0:1], b12[:, 0:1])
            dve.tensor_scalar(b2k[:, :], b12[:, 1:2], float(K), None, ALU.mult)
            w1_ba = w1_sb.rearrange("i a b -> i b a")

            def both_orders(place, a, b):
                n = (a.stop - a.start) * (b.stop - b.start)
                return dve.tensor_tensor(
                    s1[:, place:place + n].rearrange("i (a b) -> i a b", b=b.stop - b.start),
                    w1_sb[:, a, b], w1_ba[:, a, b], ALU.add)

            both_orders(CORNER, slice(0, MID0), slice(MID0, HIGH0))
            both_orders(RECT, slice(0, HIGH0), slice(HIGH0, FIELDS))
            dve.wait_ge(s1_steps, 1)
            for a, place, end in TRIANGLES:
                last = both_orders(place, slice(a, a + 1), slice(a, end))
            last.then_inc(s1_steps, 1)

            for h in range(HALVES):
                last = dve.memset(blocks[h][:, :, :, :].rearrange("p r c q -> p (r c q)"), 0.0)
            last.then_inc(zeroed, 1)
            dve.wait_ge(zeroed, 1)
            for h in range(HALVES):
                for q in range(Q):
                    dve.memset(blocks[h][q * K:(q + 1) * K, :, 0, q], 1.0)
                dve.memset(pairs[h][:, :, 0], 1.0)

            def add(to, part):
                return dve.tensor_tensor(to, to, part, ALU.add)

            def make_one_hot(i):
                size = tables[HOT[i]].shape[0] // HOT_CHUNKS
                for c in range(HOT_CHUNKS):
                    last = dve.tensor_scalar(one_hot[0:size, c, :], hot_idx[0:size, i, :], row_sb[0:size, c:c + 1],
                                             None, ALU.is_equal)
                last.then_inc(hot_ready, 1)

            def transpose(g, t, n, late=False):
                if late and n == len(GROUPS) - 1:
                    fs = slice(GATHERED[0], GATHERED[-1] + 1)
                    dve.wait_ge(late_gathered[t % 2], g * (16 * len(GATHERED)))
                else:
                    fs = slice(GROUPS[n].start, GROUPS[n].stop)
                    dve.wait_ge(gathered[t % 2][n], (g + (t // 2 + 1)) * (16 * len(GROUPS[n])))
                fk = slice(fs.start * K, fs.stop * K)
                dve.transpose(feats[:, fs, :].rearrange("p f r -> p (f r)"), rows[t % 2][:, fk])
                dve.transpose(feats_ps[:, fs, :].rearrange("p f r -> p (f r)"),
                              rows[t % 2][:, fk]).then_inc(feats_made[n], 1)

            def products(h, a, end, row):
                rs = slice(h * RH, (h + 1) * RH)
                bs = slice(HIGH0 if end == FIELDS and a < HIGH0 else a, end)
                n = bs.stop - bs.start
                return dve.tensor_tensor(
                    pairs[h][:, :, row:row + n].rearrange("p r w -> p w r"), feats_ps[:, bs, rs],
                    feats[:, a:a + 1, rs].broadcast_to([P, n, RH]), ALU.mult)

            def make_rows(h, n):
                fs = GROUPS[n]
                if n == 1:
                    for m in fs:
                        products(h, m, FIELDS, ROWS[0] + (m - MID0) * HIGHS)
                if n >= 2:
                    rs = slice(h * RH, (h + 1) * RH)
                    for q in range(Q):
                        part = slice(q * K, (q + 1) * K)
                        dve.tensor_copy(blocks[h][part, :, 1 + fs.start:1 + fs.stop, q].rearrange("p r f -> p f r"),
                                        feats_ps[part, fs.start:fs.stop, rs])
                    dve.tensor_copy(pairs[h][:, :, 1 + fs.start:1 + fs.stop].rearrange("p r w -> p w r"),
                                    feats_ps[:, fs.start:fs.stop, rs])
                for a, place, end in TRIANGLES[fs.start:fs.stop]:
                    last = products(h, a, end, place if place < ROWS[0] else place - ROW0[1] + ROWS[0])
                return last

            def tile(g, t, late=False):
                dve.wait_ge(pairs_made, g * (2 * HALVES) + HALVES * t)
                dve.wait_ge(blocks_made, g * (2 * HALVES) + HALVES * t)
                if late:
                    for i, f in enumerate(HOT):
                        hot = hot_feats[:, i, bass.ds(g * (2 * R) + (t - HOT0) * R, R)]
                        dve.tensor_copy(feats[:, f, :], hot)
                        dve.tensor_copy(feats_ps[:, f, :], hot)
                for h in range(HALVES):
                    for n in (0, 1):
                        if h == 0:
                            transpose(g, t, n, late)
                            dve.wait_ge(feats_made[n], g * 2 + (t + 1))
                        if n == 0:
                            dve.wait_ge(bank_filled, fill(g, t - 1, (h + 1) * len(FILLS) // HALVES))
                        make_rows(h, n)
                for h in range(HALVES):
                    for n in (2, 3):
                        if h == 0:
                            transpose(g, t, n, late)
                            dve.wait_ge(feats_made[n], g * 2 + (t + 1))
                        last = make_rows(h, n)
                    last.then_inc(pairs_made, 1)

            def add_dense(g, t):
                dve.wait_ge(h1_made, g * 2 + (t + 1))
                dve.tensor_tensor(h1_sb[:, :, :], h1_ps, h1_dense[:, :, bass.ds(g * (2 * P) + t * P, P)],
                                  ALU.add).then_inc(h1_added, 1)

            dve.wait_ge(hot_loaded, 16 * (1 + 2 * len(HOT)))
            make_one_hot(0)

            S, M, Z = MID0, MIDS, HIGHS
            for a in range(MID0, HIGH0):
                dve.wait_ge(u_kept, a + 1)
                add(u(0, rect_at(a, HIGH0), (US, S), (1, Z)), u(a, rect_at(0, HIGH0), (Z, S), (1, Z)))
                last = add(u(0, mid_at(a), (US, S), (1, HIGH0 - a)), u(a, corner_at(0, a), (M, S), (1, HIGH0 - a)))
            for a in range(MID0):
                last = add(u(MID0, small_at(a), (US, M), (1, S - a)), u(a, corner_at(a, MID0), (1, M), (US, S - a)))
            last.then_inc(folds, 1)
            dve.wait_ge(folds, 1)
            for a in range(MID0, HIGH0 - 1):
                add(u(0, mid_at(a) + 1, (US, S), (1, HIGH0 - a - 1)), u(a + 1, corner_at(0, a), (M, S), (US, HIGH0 - a - 1)))
            for a in range(MID0 - 1):
                add(u(MID0, small_at(a) + 1, (US, M), (1, S - a - 1)), u(a, corner_at(a + 1, MID0), (1, M), (M, S - a - 1)))
            for a in range(HIGH0, FIELDS):
                dve.wait_ge(u_kept, a + 1)
                add(u(0, high_at(a), (US, HIGH0), (1, FIELDS - a)), u(a, rect_at(0, a), (Z, HIGH0), (1, FIELDS - a)))
            for n in range(2):
                transpose(0, 0, n)
            for a in range(MID0):
                add(u(HIGH0, small_at(a), (US, Z), (1, S - a)), u(a, rect_at(a, HIGH0), (1, Z), (US, S - a)))
            for a in range(MID0, HIGH0):
                last = add(u(a, rect_at(a, HIGH0), (Z, HIGH0 - a), (1, Z)), u(HIGH0, mid_at(a), (1, HIGH0 - a), (US, Z)))
            last.then_inc(folds, 1)
            dve.wait_ge(folds, 2)
            for a in range(HIGH0, FIELDS - 1):
                add(u(0, high_at(a) + 1, (US, HIGH0), (1, FIELDS - a - 1)), u(a + 1, rect_at(0, a), (Z, HIGH0), (US, FIELDS - a - 1)))
            for a in range(MID0 - 1):
                add(u(HIGH0, small_at(a) + 1, (US, Z), (1, S - a - 1)), u(a, rect_at(a + 1, HIGH0), (1, Z), (Z, S - a - 1)))
            add(u(0, rect_at(MID0, HIGH0), (US, S), (Z, M), (1, Z)),
                u(HIGH0, corner_at(0, MID0), (M, S), (1, M), (US, Z))).then_inc(folds, 1)

            for n in range(2, len(GROUPS)):
                transpose(0, 0, n)
            for h in range(HALVES):
                for n in range(len(GROUPS)):
                    dve.wait_ge(feats_made[n], 1)
                    last = make_rows(h, n)
                last.then_inc(pairs_made, 1)
            for i in range(1, len(HOT)):
                dve.wait_ge(hot_made, i)
                make_one_hot(i)
            dve.wait_ge(dense_kept, BATCH // BANK * (TOP1 // P))
            for t in range(1, HOT0):
                tile(0, t)
                add_dense(0, t - 1)
            dve.wait_ge(hot_kept, len(HOT))
            with dve.Fori(HOT0 // 2, LOOPS) as g:
                for t in (1, 2):
                    tile(g, t, late=True)
                    add_dense(g, t - 1)
            tile(*LAST, late=True)
            add_dense(LOOPS, 0)
            for m in range(1, TOP1 // P, 2):
                dve.wait_ge(last_h1_made, m + 1)
                dve.tensor_scalar(h1_sb[:, m, :], banks[:, H1_BANKS[m], 0:P], bt1_sb[:, m:m + 1], 0.0,
                                  ALU.add, ALU.max).then_inc(last_h1_kept[m], 1)
            dve.wait_ge(last_h2_made, 2)
            dve.tensor_scalar(h2_sb[:, 1, :], banks[:, H2_BANKS[1], 0:P], bt2_sb[:, 1:2], 0.0,
                              ALU.add, ALU.max).then_inc(last_h2_kept[1], 1)

        @block.tensor
        def _(pe):
            pe.wait_ge(s1_steps, 2)
            for j in range(FIELDS):
                if j % (FIELDS // 2) == 0:
                    pe.wait_ge(w2_loaded[j // (FIELDS // 2)], 16)
                if j >= len(U_RING):
                    pe.wait_ge(u_kept, j + 1 - len(U_RING))
                pe.matmul(banks[:, U_RING[j % len(U_RING)], 0:US], w2_sb[:, j, :], s1[:, :],
                          start=True, stop=True).then_inc(u_made, 1)

            def sums_fill(g, t, k):
                c, r0 = FILLS[k]
                if c == 0 and r0 % RH == 0:
                    pe.wait_ge(blocks_made, g * 4 + (2 * t + r0 // RH + 1))
                    pe.wait_ge(pairs_made, g * 4 + (2 * t + r0 // RH + 1))
                pe.wait_ge(bank_drained, fill(g, t, k - 2))
                width = COLS[c] * Q
                for r in range(r0, r0 + RPB[c]):
                    h, at_row = r // RH, c * ROWS[0]
                    last = pe.matmul(banks[0:ROWS[c], RING[k % 3], (r - r0) * width:(r - r0 + 1) * width],
                                     pairs[h][:, r % RH, at_row:at_row + ROWS[c]],
                                     blocks[h][:, r % RH, 0:COLS[c], :].rearrange("p c q -> p (c q)"),
                                     start=True, stop=True)
                last.then_inc(bank_filled, 1)

            def z2(c):
                for unit in Z2_UNITS[c]:
                    n = z2_rows(unit)
                    last = pe.matmul(z_ps[:, 1, :], wr[0:n, unit, :], sums[0:n, unit, :],
                                     start=(unit == Z2_UNITS[0][0]), stop=(unit == Z2_UNITS[1][-1]))
                return last

            def z1(z1_ps):
                pe.matmul(z1_ps, wr[0:ROWS[0], UNIT0[0], :], sums[0:ROWS[0], UNIT0[0], :], start=True, stop=False)
                pe.matmul(z1_ps, wr[0:ONES_ROWS, UNIT0[1], :], sums[0:ONES_ROWS, UNIT0[1], :],
                          start=False, stop=False)
                n = CROSS_ROWS + REST_ROWS
                return pe.matmul(z1_ps, wr[0:n, CROSS_UNIT, :], cross[:, :], start=False, stop=True)

            def z(g, t):
                pe.wait_ge(bank_drained, fill(g, t + 1, 0))
                z2(0)
                pe.wait_ge(sums_packed, (g * 2 + (t + 1)) * (16 * (PIECES + 1)))
                z2(1)

            def z_rest(g, t):
                pe.wait_ge(cross_moved, (g * 2 + (t + 1)) * (16 * 3))
                z1(z_ps[:, 0, :]).then_inc(z_made, 1)

            def hidden1(g, t):
                pe.wait_ge(z_kept, g * 2 + (t + 1))
                for m in range(TOP1 // P):
                    ms = slice(m * P, (m + 1) * P)
                    pe.matmul(h1_ps[:, m, :], wt1_z[:, 0, ms], z_sb[:, 0, :], start=True, stop=False)
                    last = pe.matmul(h1_ps[:, m, :], wt1_z[:, 1, ms], z_sb[:, 1, :], start=False, stop=True)
                last.then_inc(h1_made, 1)

            def hidden2(g, t):
                pe.wait_ge(h1_kept, g * 2 + (t + 1))
                for m in range(TOP2 // P):
                    for c in range(TOP1 // P):
                        last = pe.matmul(h2_ps[:, m, :], wt2_sb[:, c, m * P:(m + 1) * P], h1_sb[:, c, :],
                                         start=(c == 0), stop=(c == TOP1 // P - 1))
                last.then_inc(h2_made, 1)

            def output(g, t):
                pe.wait_ge(h2_kept, g * 2 + (t + 1))
                for c in range(TOP2 // P):
                    last = pe.matmul(y_ps, wt3_sb[:, c:c + 1], h2_sb[:, c, :],
                                     start=(c == 0), stop=(c == TOP2 // P - 1))
                last.then_inc(y_made, 1)

            def tile(g, t):
                for k in range(len(FILLS)):
                    sums_fill(g, t, k)
                    if k == 2:
                        hidden1(g, t - 1)
                hidden2(g, t - 1)
                z(g, t)
                output(g, t - 1)
                z_rest(g, t)

            pe.wait_ge(ident_made, 1)
            pe.wait_ge(u_kept, FIELDS)

            def hot(i, bank):
                pe.wait_ge(hot_ready, i + 1)
                size = tables[HOT[i]].shape[0] // HOT_CHUNKS
                for c in range(HOT_CHUNKS):
                    for q in range(Q):
                        last = pe.matmul(banks[q * K:(q + 1) * K, bank, 0:HOT_N], hot_tables[i][:, c, :],
                                         one_hot[0:size, c, q * HOT_N:(q + 1) * HOT_N],
                                         start=(c == 0), stop=(c == HOT_CHUNKS - 1))
                last.then_inc(hot_made, 1)

            pe.wait_ge(hot_loaded, 16 * (1 + 2 * len(HOT)))
            hot(0, HOT_BANKS[0])
            pe.wait_ge(top_loaded, 16 * 4)
            for n, (m, b) in enumerate(DENSE_PARTS):
                if n >= len(DENSE_BANKS):
                    pe.wait_ge(dense_kept, n + 1 - len(DENSE_BANKS))
                pe.matmul(banks[:, DENSE_BANKS[n % len(DENSE_BANKS)], :], wt1_d[:, m * P:(m + 1) * P],
                          dense_sb[:, b * BANK:(b + 1) * BANK], start=True, stop=True).then_inc(dense_made, 1)
            pe.wait_ge(folds, 3)
            pe.wait_ge(hot_kept, 1)
            for k in range(TURNS):
                if k >= 3:
                    pe.wait_ge(bank_drained, k - 2)
                for unit in range(4 * k, min(4 * k + 4, UNITS)):
                    j, pair, n = weights_of(unit)
                    weights = s1[:, pair:pair + n] if j is None else u_mem[:, j, pair:pair + n]
                    last = pe.transpose(banks[0:n, RING[k % 3], (unit % 4) * H:(unit % 4 + 1) * H],
                                        weights, ident[:, :])
                last.then_inc(bank_filled, 1)
            for k in range(len(FILLS)):
                sums_fill(0, 0, k)
            pe.wait_ge(weights_moved, 16 * (PIECES + 2))
            pe.wait_ge(dense_kept, len(DENSE_PARTS))
            z(0, 0)
            z_rest(0, 0)
            for i in range(1, len(HOT)):
                hot(i, HOT_BANKS[i])
            pe.wait_ge(small_loaded, 16 * 3)
            with pe.Fori(0, LOOPS) as g:
                for t in (1, 2):
                    tile(g, t)

            g, t = LAST
            hidden1(g, t - 1)
            for k in range(len(FILLS)):
                sums_fill(g, t, k)
                if k == 5:
                    hidden2(g, t - 1)
            output(g, t - 1)
            pe.wait_ge(bank_drained, fill(g, t + 1, 0))
            z2(0)
            pe.wait_ge(cross_moved, TILES * (16 * 3))
            z1(banks[:, Z1_BANK, 0:P]).then_inc(last_z1_made, 1)
            pe.wait_ge(sums_packed, TILES * (16 * (PIECES + 1)))
            z2(1).then_inc(z_made, 1)
            pe.wait_ge(last_z1_kept, 1)
            for m, bank in enumerate(H1_BANKS):
                ms = slice(m * P, (m + 1) * P)
                pe.matmul(banks[:, bank, 0:P], wt1_z[:, 0, ms], z_sb[:, 0, :], start=True, stop=False)
                pe.matmul(banks[:, bank, 0:P], wt1_d[:, ms], dense_sb[:, BATCH - P:BATCH], start=False, stop=False)
            pe.wait_ge(z_kept, TILES)
            for m, bank in enumerate(H1_BANKS):
                pe.matmul(banks[:, bank, 0:P], wt1_z[:, 1, m * P:(m + 1) * P], z_sb[:, 1, :],
                          start=False, stop=True).then_inc(last_h1_made, 1)
            for c in range(TOP1 // P):
                pe.wait_ge(last_h1_kept[c], 1)
                for m, bank in enumerate(H2_BANKS):
                    last = pe.matmul(banks[:, bank, 0:P], wt2_sb[:, c, m * P:(m + 1) * P], h1_sb[:, c, :],
                                     start=(c == 0), stop=(c == TOP1 // P - 1))
                    if c == TOP1 // P - 1:
                        last.then_inc(last_h2_made, 1)
            for c in range(TOP2 // P):
                pe.wait_ge(last_h2_kept[c], 1)
                last = pe.matmul(y_ps, wt3_sb[:, c:c + 1], h2_sb[:, c, :],
                                 start=(c == 0), stop=(c == TOP2 // P - 1))
            last.then_inc(y_made, 1)

        @block.scalar
        def _(act):
            for j in range(FIELDS):
                act.wait_ge(u_made, j + 1)
                act.activation(u_mem[:, j, :], banks[:, U_RING[j % len(U_RING)], 0:US], ACT.Copy).then_inc(u_kept, 1)

            def make_blocks(g, t):
                act.wait_ge(upper_made, g * 2 + (t + 1))
                for h in range(HALVES):
                    for q in range(Q):
                        part = slice(q * K, (q + 1) * K)
                        last = act.activation(
                            blocks[h][part, :, 1 + MID0:COLS[0], q].rearrange("p r f -> p f r"),
                            feats[part, MID0:FIELDS, h * RH:(h + 1) * RH], ACT.Copy)
                    last.then_inc(blocks_made, 1)

            def keep_hot(i):
                act.wait_ge(hot_made, i + 1)
                act.activation(hot_feats[:, i, :], banks[:, HOT_BANKS[i], 0:HOT_N], ACT.Copy).then_inc(hot_kept, 1)

            def drain(g, t, k):
                c, r0 = FILLS[k]
                act.wait_ge(bank_filled, fill(g, t, k + 1))
                act.activation(
                    sums[0:ROWS[c], UNIT0[c]:UNIT0[c] + COLS[c], r0 * Q:(r0 + RPB[c]) * Q].rearrange(
                        "w c (r q) -> w c r q", q=Q),
                    banks[0:ROWS[c], RING[k % 3], 0:RPB[c] * COLS[c] * Q].rearrange(
                        "w (r c q) -> w c r q", r=RPB[c], q=Q), ACT.Copy).then_inc(bank_drained, 1)

            def keep_z(g, t):
                act.wait_ge(z_made, g * 2 + (t + 1))
                act.activation(z_sb[:, 0, :], z_ps[:, 0, :], ACT.Copy)
                act.activation(z_sb[:, 1, :], z_ps[:, 1, :], ACT.Identity, bias=b2k[:, :]).then_inc(z_kept, 1)

            def keep_h1(g, t):
                act.wait_ge(h1_added, g * 2 + (t + 1))
                act.activation(h1_sb[:, :, :], h1_sb[:, :, :], ACT.Relu).then_inc(h1_kept, 1)

            def keep_h2(g, t):
                act.wait_ge(h2_made, g * 2 + (t + 1))
                for m in range(TOP2 // P):
                    last = act.activation(h2_sb[:, m, :], h2_ps[:, m, :], ACT.Relu, bias=bt2_sb[:, m:m + 1])
                last.then_inc(h2_kept, 1)

            def keep_y(g, t):
                act.wait_ge(y_made, g * 2 + (t + 1))
                act.activation(y_sb[:, bass.ds(g * (2 * P) + t * P, P)], y_ps, ACT.Copy).then_inc(y_kept, 1)

            def tile(g, t):
                keep_z(g, t - 1)
                for k in range(len(FILLS)):
                    drain(g, t, k)
                    if k == 2:
                        keep_h1(g, t - 1)
                keep_h2(g, t - 1)
                make_blocks(g, t + 1)
                keep_y(g, t - 1)

            act.wait_ge(zeroed, 1)
            keep_hot(0)
            act.wait_ge(small_loaded, 16 * 3)
            for n, (m, b) in enumerate(DENSE_PARTS):
                if n == len(DENSE_PARTS) // 2:
                    make_blocks(0, 0)
                act.wait_ge(dense_made, n + 1)
                act.activation(h1_dense[:, m, b * BANK:(b + 1) * BANK], banks[:, DENSE_BANKS[n % len(DENSE_BANKS)], :],
                               ACT.Identity, bias=bt1_sb[:, m:m + 1]).then_inc(dense_kept, 1)
            for k in range(TURNS):
                act.wait_ge(bank_filled, k + 1)
                units = range(4 * k, min(4 * k + 4, UNITS))
                for n in sorted({weights_of(unit)[2] for unit in units}):
                    same = [unit for unit in units if weights_of(unit)[2] == n]
                    last = act.activation(
                        wr[0:n, same[0]:same[-1] + 1, :].rearrange("w u h -> w (u h)"),
                        banks[0:n, RING[k % 3], (same[0] % 4) * H:(same[-1] % 4 + 1) * H], ACT.Copy)
                last.then_inc(bank_drained, 1)
            for k in range(len(FILLS)):
                drain(0, 0, k)
            make_blocks(0, 1)
            for i in range(1, len(HOT)):
                keep_hot(i)
            with act.Fori(0, LOOPS) as g:
                for t in (1, 2):
                    tile(g, t)

            g, t = LAST
            keep_z(g, t - 1)
            for k in range(len(FILLS)):
                drain(g, t, k)
                if k == 2:
                    keep_h1(g, t - 1)
                elif k == 5:
                    keep_h2(g, t - 1)
            keep_y(g, t - 1)
            act.wait_ge(last_z1_made, 1)
            act.activation(z_sb[:, 0, :], banks[:, Z1_BANK, 0:P], ACT.Copy).then_inc(last_z1_kept, 1)
            act.wait_ge(z_made, TILES)
            act.activation(z_sb[:, 1, :], z_ps[:, 1, :], ACT.Identity, bias=b2k[:, :]).then_inc(z_kept, 1)
            for m in range(0, TOP1 // P, 2):
                act.wait_ge(last_h1_made, m + 1)
                act.activation(h1_sb[:, m, :], banks[:, H1_BANKS[m], 0:P], ACT.Relu,
                               bias=bt1_sb[:, m:m + 1]).then_inc(last_h1_kept[m], 1)
            act.wait_ge(last_h2_made, 1)
            act.activation(h2_sb[:, 0, :], banks[:, H2_BANKS[0], 0:P], ACT.Relu,
                           bias=bt2_sb[:, 0:1]).then_inc(last_h2_kept[0], 1)
            act.wait_ge(y_made, TILES)
            act.activation(y_sb[:, BATCH - P:BATCH], y_ps, ACT.Copy).then_inc(y_kept, 1)


def kernel(**inputs):
    import numpy as np
    import concourse.bacc as bacc
    from concourse.bass_utils import run_bass_kernel_spmd as run

    x = {name: np.asarray(a) for name, a in inputs.items()}
    ids = x["ids"].reshape(TILES, R, Q, FIELDS).transpose(0, 2, 1, 3).reshape(BATCH, FIELDS)
    hot_ids = ids.reshape(TILES, Q, R, FIELDS)[HOT0:, :, :, list(HOT)].transpose(3, 1, 0, 2).reshape(len(HOT), -1)
    table_row = np.arange(P * HOT_CHUNKS, dtype=np.float32).reshape(P, HOT_CHUNKS)
    arrays = {"ids": ids, "hot_ids": hot_ids, "table_row": table_row}
    for f in range(FIELDS):
        arrays[f"tbl_{f}"] = x[f"tbl_{f}"]
    arrays |= {
        "dense_t": x["dense_ctx"].T,
        "w1": x["L0_rec_W1"].reshape(H, PAIRS),
        "w2_t": x["L0_rec_W2"].transpose(1, 2, 0).reshape(H, FIELDS * H),
        "b1": x["L0_rec_b1"].reshape(H, 1),
        "b2": x["L0_rec_b2"].reshape(H, 1),
        "wt1": x["W_top1"],
        "bt1": x["b_top1"].reshape(TOP1 // P, P).T,
        "wt2": x["W_top2"],
        "bt2": x["b_top2"].reshape(TOP2 // P, P).T,
        "wt3": x["W_top3"].reshape(TOP2 // P, P).T,
    }
    arrays = {name: np.ascontiguousarray(a) for name, a in arrays.items()}
    nc = bacc.Bacc("TRN2", target_bir_lowering=False, num_devices=1)
    aps = {n: nc.dram_tensor(f"in_{n}", a.shape, mybir.dt.from_np(a.dtype), kind="ExternalInput").ap()
           for n, a in arrays.items()}
    out = nc.dram_tensor("out_y", (1, BATCH), F32, kind="ExternalOutput").ap()
    tables = [aps.pop(f"tbl_{f}") for f in range(FIELDS)]
    dlrm_tower(nc, tables=tables, out=out, **aps)
    r = run(nc, [{f"in_{n}": a for n, a in arrays.items()}], core_ids=[0])
    return r.results[0]["out_y"].reshape(BATCH, 1)
```
